# Optimizing a Trainium2 kernel written in Bass

```python
import numpy as np
import jax
import jax.numpy as jnp

def _softmax(x, axis=-1):
    return jax.nn.softmax(x, axis=axis)

def _gelu(x):
    return jax.nn.gelu(x, approximate=True)

def _silu(x):
    return jax.nn.silu(x)

def _sigmoid(x):
    return jax.nn.sigmoid(x)

def _layernorm(x, axis=-1, eps=1e-05):
    m = jnp.mean(x, axis=axis, keepdims=True)
    v = jnp.var(x, axis=axis, keepdims=True)
    return (x - m) / jnp.sqrt(v + eps)

def _scatter_add(tgt, idx, src, axis=0):
    return tgt.at[idx].add(src)

def _segment_sum(src, seg, n):
    return jax.ops.segment_sum(src, seg, n)
kernel_name = 'mk_seq_preln_d1_jaxref_r4_326486'

def setup_inputs(seed: int=0):
    np.random.seed(seed)
    _w = jnp.asarray

    def _L0_attn_setup():
        import jax, jax.numpy as jnp
        import numpy as np
        H = 16
        HD = 128
        BS = 64
        SEL = 8
        WIN = 64
        BASE = 10000.0

        def _rope(t):
            n, hd = (t.shape[1], t.shape[-1])
            half = hd // 2
            inv = 1.0 / BASE ** (jnp.arange(half, dtype=jnp.float32) / half)
            th = jnp.arange(n, dtype=jnp.float32)[:, None] * inv[None, :]
            cos = jnp.cos(th)[None, :, None, :]
            sin = jnp.sin(th)[None, :, None, :]
            t1, t2 = (t[..., :half], t[..., half:])
            return jnp.concatenate([t1 * cos - t2 * sin, t1 * sin + t2 * cos], axis=-1)

        def _nsa_forward(x, Wq, Wk, Wv, Wg, Wo):
            b, n, d = x.shape
            nb = n // BS
            scale = HD ** (-0.5)
            q = (x @ Wq).reshape(b, n, H, HD)
            k = (x @ Wk).reshape(b, n, H, HD)
            v = (x @ Wv).reshape(b, n, H, HD)
            g = jax.nn.sigmoid(x @ Wg)
            g_cmp, g_slc, g_swa = jnp.split(g, 3, axis=-1)
            q = _rope(q)
            k = _rope(k)
            idx = jnp.arange(n)
            k_cmp = k.reshape(b, nb, BS, H, HD).mean(axis=2)
            v_cmp = v.reshape(b, nb, BS, H, HD).mean(axis=2)
            s_cmp = jnp.einsum('bnhd,bmhd->bhnm', q, k_cmp) * scale
            blk_end = (jnp.arange(nb) + 1) * BS - 1
            cmp_mask = idx[:, None] >= blk_end[None, :]
            p_cmp = jax.nn.softmax(jnp.where(cmp_mask[None, None], s_cmp, -1e+30), axis=-1)
            p_cmp = p_cmp * cmp_mask.any(-1)[None, None, :, None]
            o_cmp = jnp.einsum('bhnm,bmhd->bnhd', p_cmp, v_cmp)
            cur_blk = jax.nn.one_hot(idx // BS, nb, dtype=jnp.float32)
            imp = p_cmp + 2.0 * cur_blk[None, None]
            sel = jax.lax.top_k(imp, SEL)[1]
            blk_sel = jax.nn.one_hot(sel, nb).sum(-2) > 0
            causal = idx[:, None] >= idx[None, :]
            slc_mask = blk_sel[..., idx // BS] & causal[None, None]
            s_full = jnp.einsum('bnhd,bmhd->bhnm', q, k) * scale
            p_slc = jax.nn.softmax(jnp.where(slc_mask, s_full, -1e+30), axis=-1)
            o_slc = jnp.einsum('bhnm,bmhd->bnhd', p_slc, v)
            swa_mask = causal & (idx[:, None] - idx[None, :] <= WIN)
            p_swa = jax.nn.softmax(jnp.where(swa_mask[None, None], s_full, -1e+30), axis=-1)
            o_swa = jnp.einsum('bhnm,bmhd->bnhd', p_swa, v)
            o = o_cmp * g_cmp[..., None] + o_slc * g_slc[..., None] + o_swa * g_swa[..., None]
            return o.reshape(b, n, H * HD) @ Wo
        key = jax.random.key(seed)
        ks = jax.random.split(key, 6)
        B, N, D = (2, 256, 512)
        std = 0.02
        return {'x': jax.random.normal(ks[0], (B, N, D), jnp.float32), 'Wq': jax.random.normal(ks[1], (D, H * HD), jnp.float32) * std, 'Wk': jax.random.normal(ks[2], (D, H * HD), jnp.float32) * std, 'Wv': jax.random.normal(ks[3], (D, H * HD), jnp.float32) * std, 'Wg': jax.random.normal(ks[4], (D, 3 * H), jnp.float32) * std, 'Wo': jax.random.normal(ks[5], (H * HD, D), jnp.float32) * std}
    _L0_attn_in = _L0_attn_setup()

    def _L0_ffn_setup():
        import jax, jax.numpy as jnp
        import numpy as np
        B, S, D = (4, 1024, 512)
        DFF = 4 * D
        CAPACITY = 0.125
        K = int(CAPACITY * S)
        key = jax.random.key(seed)
        ks = jax.random.split(key, 8)
        sc = 1.0 / np.sqrt(D)
        return {'x': jax.random.normal(ks[0], (B, S, D), dtype=jnp.float32), 'W_r': jax.random.normal(ks[1], (D, 1), dtype=jnp.float32) * sc, 'b_r': jnp.zeros((1,), dtype=jnp.float32), 'W1': jax.random.normal(ks[2], (D, DFF), dtype=jnp.float32) * sc, 'b1': jnp.zeros((DFF,), dtype=jnp.float32), 'W2': jax.random.normal(ks[3], (DFF, D), dtype=jnp.float32) * (1.0 / np.sqrt(DFF)), 'b2': jnp.zeros((D,), dtype=jnp.float32), 'position_ids': jnp.arange(B * S, dtype=jnp.int64 if jax.config.jax_enable_x64 else jnp.int32).reshape(B, S), 'cache_position': jnp.arange(S, dtype=jnp.int64 if jax.config.jax_enable_x64 else jnp.int32)}
    _L0_ffn_in = _L0_ffn_setup()
    _d = {'L0_attn_x': _L0_attn_in['x'], 'L0_attn_Wq': _L0_attn_in['Wq'], 'L0_attn_Wk': _L0_attn_in['Wk'], 'L0_attn_Wv': _L0_attn_in['Wv'], 'L0_attn_Wg': _L0_attn_in['Wg'], 'L0_attn_Wo': _L0_attn_in['Wo'], 'L0_ffn_W_r': _L0_ffn_in['W_r'], 'L0_ffn_b_r': _L0_ffn_in['b_r'], 'L0_ffn_W1': _L0_ffn_in['W1'], 'L0_ffn_b1': _L0_ffn_in['b1'], 'L0_ffn_W2': _L0_ffn_in['W2'], 'L0_ffn_b2': _L0_ffn_in['b2'], 'L0_ffn_position_ids': _L0_ffn_in['position_ids'], 'L0_ffn_cache_position': _L0_ffn_in['cache_position']}
    _x0 = _d['L0_attn_x']
    _d['L0_attn_x'] = jax.random.normal(jax.random.fold_in(jax.random.key(seed), 1), (8, 512, 512), dtype=_x0.dtype)
    del _x0
    return _d

def reference(L0_attn_x, L0_attn_Wq, L0_attn_Wk, L0_attn_Wv, L0_attn_Wg, L0_attn_Wo, L0_ffn_W_r, L0_ffn_b_r, L0_ffn_W1, L0_ffn_b1, L0_ffn_W2, L0_ffn_b2, L0_ffn_position_ids, L0_ffn_cache_position):

    def _L0_attn_ref(x, Wq, Wk, Wv, Wg, Wo):
        import jax, jax.numpy as jnp
        import numpy as np
        H = 16
        HD = 128
        BS = 64
        SEL = 8
        WIN = 64
        BASE = 10000.0

        def _rope(t):
            n, hd = (t.shape[1], t.shape[-1])
            half = hd // 2
            inv = 1.0 / BASE ** (jnp.arange(half, dtype=jnp.float32) / half)
            th = jnp.arange(n, dtype=jnp.float32)[:, None] * inv[None, :]
            cos = jnp.cos(th)[None, :, None, :]
            sin = jnp.sin(th)[None, :, None, :]
            t1, t2 = (t[..., :half], t[..., half:])
            return jnp.concatenate([t1 * cos - t2 * sin, t1 * sin + t2 * cos], axis=-1)

        def _nsa_forward(x, Wq, Wk, Wv, Wg, Wo):
            b, n, d = x.shape
            nb = n // BS
            scale = HD ** (-0.5)
            q = (x @ Wq).reshape(b, n, H, HD)
            k = (x @ Wk).reshape(b, n, H, HD)
            v = (x @ Wv).reshape(b, n, H, HD)
            g = jax.nn.sigmoid(x @ Wg)
            g_cmp, g_slc, g_swa = jnp.split(g, 3, axis=-1)
            q = _rope(q)
            k = _rope(k)
            idx = jnp.arange(n)
            k_cmp = k.reshape(b, nb, BS, H, HD).mean(axis=2)
            v_cmp = v.reshape(b, nb, BS, H, HD).mean(axis=2)
            s_cmp = jnp.einsum('bnhd,bmhd->bhnm', q, k_cmp) * scale
            blk_end = (jnp.arange(nb) + 1) * BS - 1
            cmp_mask = idx[:, None] >= blk_end[None, :]
            p_cmp = jax.nn.softmax(jnp.where(cmp_mask[None, None], s_cmp, -1e+30), axis=-1)
            p_cmp = p_cmp * cmp_mask.any(-1)[None, None, :, None]
            o_cmp = jnp.einsum('bhnm,bmhd->bnhd', p_cmp, v_cmp)
            cur_blk = jax.nn.one_hot(idx // BS, nb, dtype=jnp.float32)
            imp = p_cmp + 2.0 * cur_blk[None, None]
            sel = jax.lax.top_k(imp, SEL)[1]
            blk_sel = jax.nn.one_hot(sel, nb).sum(-2) > 0
            causal = idx[:, None] >= idx[None, :]
            slc_mask = blk_sel[..., idx // BS] & causal[None, None]
            s_full = jnp.einsum('bnhd,bmhd->bhnm', q, k) * scale
            p_slc = jax.nn.softmax(jnp.where(slc_mask, s_full, -1e+30), axis=-1)
            o_slc = jnp.einsum('bhnm,bmhd->bnhd', p_slc, v)
            swa_mask = causal & (idx[:, None] - idx[None, :] <= WIN)
            p_swa = jax.nn.softmax(jnp.where(swa_mask[None, None], s_full, -1e+30), axis=-1)
            o_swa = jnp.einsum('bhnm,bmhd->bnhd', p_swa, v)
            o = o_cmp * g_cmp[..., None] + o_slc * g_slc[..., None] + o_swa * g_swa[..., None]
            return o.reshape(b, n, H * HD) @ Wo
        return _nsa_forward(x, Wq, Wk, Wv, Wg, Wo)

    def _L0_ffn_ref(x, W_r, b_r, W1, b1, W2, b2, position_ids, cache_position):
        import jax, jax.numpy as jnp
        import numpy as np
        B, S, D = (4, 1024, 512)
        DFF = 4 * D
        CAPACITY = 0.125
        K = int(CAPACITY * S)
        b, s, d = x.shape
        weights = jnp.einsum('bsd,do->bso', x, W_r).squeeze(-1) + b_r
        topk_vals, topk_idx = jax.lax.top_k(weights, K)
        threshold = topk_vals[:, -1]
        sel_mask = weights > threshold[:, None]
        xg = jnp.take_along_axis(x, topk_idx[..., None], axis=1)
        h = jax.nn.gelu(jnp.einsum('bkd,df->bkf', xg, W1) + b1)
        blk = jnp.einsum('bkf,fd->bkd', h, W2) + b2
        gate = (topk_vals > threshold[:, None]).astype(x.dtype)
        wg = jnp.take_along_axis(weights, topk_idx, axis=1)
        vals = blk * (wg * gate)[..., None]
        bidx = jnp.arange(b)[:, None]
        processed = jnp.zeros_like(x).at[bidx, topk_idx].add(vals)
        return processed + x * (~sel_mask)[..., None].astype(x.dtype)
    x = L0_attn_x
    x = x + _L0_attn_ref(_layernorm(x, axis=-1), L0_attn_Wq, L0_attn_Wk, L0_attn_Wv, L0_attn_Wg, L0_attn_Wo)
    x = x + _L0_ffn_ref(_layernorm(x, axis=-1), L0_ffn_W_r, L0_ffn_b_r, L0_ffn_W1, L0_ffn_b1, L0_ffn_W2, L0_ffn_b2, L0_ffn_position_ids, L0_ffn_cache_position)
    return x

_drawn_inputs = setup_inputs


def setup_inputs(seed=0):
    import zlib

    import numpy as np

    out = dict(_drawn_inputs(seed))
    spreads = {'L0_ffn_b1': (0.0, 0.288), 'L0_ffn_b2': (0.0, 0.1)}
    factors = {}
    for name, (base, spread) in spreads.items():
        noise = np.random.default_rng([zlib.crc32(name.encode()), seed]).standard_normal(out[name].shape)
        drawn = base * np.exp(spread * noise) if base else spread * noise
        out[name] = jnp.asarray(drawn.astype(out[name].dtype))
    for name, factor in factors.items():
        out[name] = (out[name] * factor).astype(out[name].dtype)
    return out
```

```python
import numpy as np
import concourse.bass as bass
from concourse import mybir
from concourse.alu_op_type import AluOpType as ALU

B, N, D = 8, 512, 512
H, HD = 16, 128
BS = 64
NB = N // BS
WIN = 64
DFF = 4 * 512
KTOP = int(0.125 * 1024)
EPS = 1e-5
NEG = -1e30
P = 128
T = N // P
C = D // P
FT = DFF // P
BASE = 10000.0

F32, F32R, BF16 = mybir.dt.float32, mybir.dt.float32r, mybir.dt.bfloat16
ACT = mybir.ActivationFunctionType
AX = mybir.AxisListType

E1OFF = [0, 128, 384, 768]
E1W = 1280
PTOFF = [0, 512, 896, 1152]
PTQ0 = [0, 128, 256, 256]
PTW = 1408


def consts():
    half = HD // 2
    inv = (np.float32(1.0) / np.float32(BASE) ** (np.arange(half, dtype=np.float32) / np.float32(half))).astype(np.float32)
    th = (np.arange(N, dtype=np.float32)[:, None] * inv[None, :]).astype(np.float32)
    cos, sin = np.cos(th).T.astype(np.float32), np.sin(th).T.astype(np.float32)
    cosk = np.concatenate([cos, cos])
    sink = np.concatenate([-sin, sin])
    scale = np.float32(HD ** -0.5)
    rope = np.stack([cosk * scale, sink * scale, cosk, sink], 1)
    p = np.arange(P)
    ident = np.eye(P)
    causal = np.where(p[None, :] <= p[:, None], 0.0, NEG)
    c = np.arange(P + WIN)
    window = np.where((c[None, :] <= p[:, None] + WIN) & (c[None, :] >= p[:, None]), 0.0, NEG)
    q = p[:, None] + P * np.arange(T)[None, :]
    ends = (np.arange(NB) + 1) * BS - 1
    cmask = np.where(q[:, :, None] >= ends, 0.0, NEG)
    some = (q >= ends[0]) / BS
    before = np.where(p[:, None] < p[None, :], 1.0, 0.0)
    slot = np.broadcast_to(p[None, :], (P, P))
    ones = np.ones((P, P))
    misc = np.concatenate([x.reshape(P, -1) for x in (ident, causal, window, cmask, some, before, slot, ones)], 1)
    return rope.reshape(P, -1).astype(np.float32), misc.astype(np.float32)


MISC = {}
_at = 0
for _n, _w in (("ident", P), ("causal", P), ("window", P + WIN), ("cmask", T * NB), ("some", T), ("before", P), ("slot", P), ("ones", P)):
    MISC[_n] = (_at, _at + _w)
    _at += _w
MISCW = _at


class Region:

    def __init__(self, nc, at):
        self.nc, self.at = nc, at

    def __call__(self, name, shape, dt=F32):
        n = 4 if dt != BF16 else 2
        for s in shape[1:]:
            n *= s
        t = self.nc.alloc_sbuf_tensor_at(name, shape, dt, offset=self.at)
        self.at += -(-n // 32) * 32
        return t


def f32(ap):
    return ap.bitcast(F32)


def build(nc, x, wq, wk, wv, wg, wo, wr, br, w1, b1, w2, b2, rope_d, misc_d, out, stop=9):
    keep = Region(nc, -(-nc.sbuf_base // 32) * 32)
    misc = keep("misc", [P, MISCW])
    ident_b = keep("ident_b", [P, P], BF16)
    causal_b = keep("causal_b", [P, P], BF16)
    rows_at = keep.at
    gates = keep("gates", [P, B, H, 3, T])
    xt_hi = keep("xt_hi", [P, B, C, N], F32R)
    xt_lo = keep("xt_lo", [P, B, C, N], F32R)
    phase = keep.at
    banks = [nc.alloc_psum_tensor(f"bank{i}", [P, 512], F32) for i in range(8)]
    o_dram = nc.dram_tensor("o_scratch", [B, P, H, N], F32, kind="Internal").ap()

    def m(name):
        a, b = MISC[name]
        return misc[:, a:b]

    normalise(nc, phase, banks, misc, m, ident_b, causal_b, gates, xt_hi, xt_lo, x, wg, misc_d)
    attend(nc, phase, banks, m, ident_b, causal_b, gates, xt_hi, xt_lo, wq, wk, wv, rope_d, o_dram)
    feed_forward(nc, rows_at, banks, m, o_dram, x, wo, wr, br, w1, b1, w2, b2, out)


def normalise(nc, phase, banks, misc, m, ident_b, causal_b, gates, xt_hi, xt_lo, x, wg, misc_d):
    r = Region(nc, phase)
    xin = r("xin", [P, 2, T, D])
    z = r("z", [P, T, D])
    stats = r("stats", [P, T, 6])
    mv = r("mv", [P, T, 2])
    ve = r("ve", [P, T])
    sd = r("sd", [P, T])
    y = r("y", [P, T])
    yy = r("yy", [P, T])
    ge = r("ge", [P, N])
    gs = r("gs", [P, T, 3 * H])
    wg_raw = r("wg_raw", [P, C, P])
    wg_hi = r("wg_hi", [P, C, P], F32R)
    wg_lo = r("wg_lo", [P, C, P], F32R)
    S = nc.alloc_semaphore
    misc_loaded, wg_zeroed, wg_loaded = S("misc_loaded"), S("wg_zeroed"), S("wg_loaded")
    x_loaded = [S("x_loaded0"), S("x_loaded1")]
    wg_split, masks_ready = S("wg_split"), S("masks_ready")
    stat_step, sd_ready, z_ready, xt_transposed = S("stat_step"), S("sd_ready"), S("z_ready"), S("xt_transposed")
    xt_hi_ready, xt_lo_ready, g_projected, g_exp = S("xt_hi_ready"), S("xt_lo_ready"), S("g_projected"), S("g_exp")
    g_transposed, g_step = S("g_transposed"), S("g_step")
    NSTAT, NG = 4 + 4 + 1 + 5, T + 3

    with nc.Block() as block:
        @block.sync
        def _(sp):
            sp.dma_start(misc[:], misc_d).then_inc(misc_loaded, 16)
            for b in range(B):
                if b >= 2:
                    sp.wait_ge(z_ready, T * (b - 1))
                sp.dma_start(xin[:, b % 2], x[b].rearrange("(t p) d -> p t d", p=P)).then_inc(x_loaded[b % 2], 16)
                if b == 0:
                    sp.wait_ge(wg_zeroed, 1)
                    sp.dma_start(wg_raw[:, :, 0:3 * H], wg.rearrange("(c p) n -> p c n", p=P)).then_inc(wg_loaded, 16)

        @block.gpsimd
        def _(pool):
            nc.gpsimd.memset(wg_raw[:], 0.0).then_inc(wg_zeroed, 1)

        @block.vector
        def _(dve):
            dve.wait_ge(misc_loaded, 16)
            nc.vector.tensor_copy(ident_b[:], m("ident")).then_inc(masks_ready, 1)
            nc.vector.tensor_copy(causal_b[:], m("causal")).then_inc(masks_ready, 1)
            dve.wait_ge(wg_loaded, 16)
            nc.vector.tensor_copy(wg_hi[:], wg_raw[:]).then_inc(wg_split, 1)
            dve.wait_ge(wg_split, 1)
            nc.vector.tensor_tensor(wg_lo[:], wg_raw[:], f32(wg_hi[:]), ALU.subtract).then_inc(wg_split, 1)
            with dve.Fori(0, B // 2) as pair:
                for s in range(2):
                    b = pair * 2 + s
                    dve.wait_ge(x_loaded[s], pair * 16 + 16)
                    for t in range(T):
                        nc.vector.bn_stats(stats[:, t], xin[:, s, t]).then_inc(stat_step, 1)
                    dve.wait_ge(stat_step, b * NSTAT + 4)
                    nc.vector.memset(yy[:], 0.0)
                    for t in range(T):
                        nc.vector.bn_aggr(mv[:, t], stats[:, t]).then_inc(stat_step, 1)
                    dve.wait_ge(stat_step, b * NSTAT + 8)
                    nc.vector.tensor_scalar(ve[:], mv[:, :, 1], EPS, None, ALU.add).then_inc(stat_step, 1)
                    dve.wait_ge(sd_ready, b + 1)
                    nc.vector.reciprocal(y[:], sd[:]).then_inc(stat_step, 1)
                    dve.wait_ge(stat_step, b * NSTAT + 10)
                    nc.vector.tensor_tensor(yy[:], y[:], y[:], ALU.mult).then_inc(stat_step, 1)
                    dve.wait_ge(stat_step, b * NSTAT + 11)
                    nc.vector.tensor_tensor(yy[:], yy[:], ve[:], ALU.mult).then_inc(stat_step, 1)
                    dve.wait_ge(stat_step, b * NSTAT + 12)
                    nc.vector.tensor_scalar(yy[:], yy[:], -0.5, 1.5, ALU.mult, ALU.add).then_inc(stat_step, 1)
                    dve.wait_ge(stat_step, b * NSTAT + 13)
                    nc.vector.tensor_tensor(y[:], yy[:], y[:], ALU.mult).then_inc(stat_step, 1)
                    dve.wait_ge(stat_step, b * NSTAT + 14)
                    for t in range(T):
                        nc.vector.tensor_scalar(z[:, t], xin[:, s, t], mv[:, t, 0:1], y[:, t:t + 1],
                                                ALU.subtract, ALU.mult).then_inc(z_ready, 1)
                    for c in range(C):
                        dve.wait_ge(xt_hi_ready, b * C + c + 1)
                        nc.vector.tensor_tensor(xt_lo[:, bass.ds(b, 1), c, :], banks[c][:, :],
                                                f32(xt_hi[:, bass.ds(b, 1), c, :]), ALU.subtract).then_inc(xt_lo_ready, 1)
                    dve.wait_ge(g_transposed, b + 1)
                    nc.vector.tensor_scalar(gs[:], banks[5][:, :].rearrange("p (t n) -> p t n", t=T)[:, :, 0:3 * H],
                                            1.0, None, ALU.add).then_inc(g_step, 1)
                    dve.wait_ge(g_step, b * NG + 1)
                    nc.vector.reciprocal(gs[:], gs[:]).then_inc(g_step, 1)
                    dve.wait_ge(g_step, b * NG + 2)
                    for t in range(T):
                        nc.vector.tensor_scalar(gates[:, bass.ds(b, 1), :, :, t].rearrange("p o h r -> p o r h"),
                                                gs[:, t:t + 1].rearrange("p o (r h) -> p o r h", r=3),
                                                1.0, None, ALU.mult).then_inc(g_step, 1)
                    dve.wait_ge(g_step, b * NG + T + 2)
                    gc = gates[:, bass.ds(b, 1), :, 0, :]
                    nc.vector.tensor_tensor(gc, gc, m("some").rearrange("p (o a t) -> p o a t", o=1, a=1).to_broadcast([P, 1, H, T]),
                                            ALU.mult).then_inc(g_step, 1)

        @block.scalar
        def _(act):
            with act.Fori(0, B // 2) as pair:
                for s in range(2):
                    b = pair * 2 + s
                    act.wait_ge(stat_step, b * NSTAT + 9)
                    nc.scalar.activation(sd[:], ve[:], ACT.Sqrt).then_inc(sd_ready, 1)
                    for c in range(C):
                        act.wait_ge(xt_transposed, b * C + c + 1)
                        nc.scalar.activation(xt_hi[:, bass.ds(b, 1), c, :], banks[c][:, :], ACT.Copy).then_inc(xt_hi_ready, 1)
                    act.wait_ge(g_projected, b + 1)
                    nc.scalar.activation(ge[:, :], banks[4][:, :], ACT.Exp, scale=-1.0).then_inc(g_exp, 1)

        @block.tensor
        def _(pe):
            pe.wait_ge(misc_loaded, 16)
            pe.wait_ge(wg_split, 2)
            with pe.Fori(0, B // 2) as pair:
                for s in range(2):
                    b = pair * 2 + s
                    pe.wait_ge(z_ready, b * T + T)
                    for c in range(C):
                        for t in range(T):
                            last = nc.tensor.transpose(banks[c][:, t * P:(t + 1) * P], z[:, t, c * P:(c + 1) * P], m("ident"))
                        last.then_inc(xt_transposed, 1)
                    pe.wait_ge(xt_lo_ready, b * C + C)
                    for c in range(C):
                        for w, v in ((wg_hi, xt_hi), (wg_hi, xt_lo), (wg_lo, xt_hi)):
                            last = nc.tensor.matmul(banks[4][:, :], w[:, c, :], v[:, bass.ds(b, 1), c, :],
                                                    start=(c == 0 and w is wg_hi and v is xt_hi), stop=(c == C - 1 and w is wg_lo))
                    last.then_inc(g_projected, 1)
                    pe.wait_ge(g_exp, b + 1)
                    for t in range(T):
                        last = nc.tensor.transpose(banks[5][:, t * P:(t + 1) * P], ge[:, t * P:(t + 1) * P], m("ident"))
                    last.then_inc(g_transposed, 1)


def attend(nc, phase, banks, m, ident_b, causal_b, gates, xt_hi, xt_lo, wq, wk, wv, rope_d, o_dram):
    r = Region(nc, phase)
    rope = r("rope", [P, 4, N])
    w_raw = [r(f"w_raw{k}", [P, C, HD]) for k in range(3)]
    w_hi = [r(f"w_hi{k}", [P, C, HD], F32R) for k in range(3)]
    w_lo = [r(f"w_lo{k}", [P, C, HD], F32R) for k in range(3)]
    s_full = [r(f"s_full{k}", [P, N]) for k in range(2)]
    s_swap = [r(f"s_swap{k}", [P, N]) for k in range(2)]
    qk_hi = [r(f"qk_hi{k}", [P, N], F32R) for k in range(2)]
    qk_lo = [r(f"qk_lo{k}", [P, N], F32R) for k in range(2)]
    vt = r("vt", [P, N])
    v_hi = r("v_hi", [P, T, HD], F32R)
    v_lo = r("v_lo", [P, T, HD], F32R)
    e1 = r("e1", [P, E1W])
    e2 = r("e2", [P, T, P + WIN])
    pt_hi = r("pt_hi", [P, PTW], F32R)
    pt_lo = r("pt_lo", [P, PTW], F32R)
    o_sb = r("o_sb", [P, N])
    neg1 = r("neg1", [P, T])
    max2 = r("max2", [P, T])
    neg2 = r("neg2", [P, T])
    sc = r("sc", [P, T, NB])
    sc2 = r("sc2", [P, T, NB])
    mc = r("mc", [P, T])
    sums = r("sums", [P, 3, T])
    coef = r("coef", [P, 3, T])
    cb = r("cb", [P, T, NB])
    assert r.at <= nc.sbuf_usable_end, r.at

    S = nc.alloc_semaphore
    rope_loaded = S("rope_loaded")
    w_loaded = [S(f"w{k}_loaded") for k in range(3)]
    w_split = [S(f"w{k}_split") for k in range(3)]
    projected = [S(f"{k}_projected") for k in "qkv"]
    evacuated = [S(f"{k}_evacuated") for k in "qkv"]
    swapped = [S("q_swapped"), S("k_swapped")]
    cos_done = [S("q_cos"), S("k_cos")]
    sin_done = [S("q_sin"), S("k_sin")]
    roped = [S("q_roped"), S("k_roped")]
    hi_done = [S("q_hi_done"), S("k_hi_done")]
    lo_done = [S("q_lo_done"), S("k_lo_done")]
    v_transposed, v_hi_done, v_lo_done = S("v_transposed"), S("v_hi_done"), S("v_lo_done")
    scores_ready, negmax, window_masked, negmax2 = S("scores_ready"), S("negmax"), S("window_masked"), S("negmax2")
    cmp_step, exp_cmp, exp_full, exp_win = S("cmp_step"), S("exp_cmp"), S("exp_full"), S("exp_win")
    mixed, probs_ready = S("mixed"), S("probs_ready")
    pt_ready, pt_hi_done, pt_lo_done = S("pt_ready"), S("pt_hi_done"), S("pt_lo_done")
    out_ready, out_evacuated, out_slot_free, zeros_set = S("out_ready"), S("out_evacuated"), S("out_slot_free"), S("zeros_set")
    NC = T + 3 + 4
    w_dram = [w.rearrange("(c p) n -> p c n", p=P) for w in (wq, wk, wv)]
    QB = [4, 5, 4]

    def units(eng, body, start=lambda h: None):
        with eng.Fori(0, H - 1) as h:
            start(h)
            with eng.Fori(0, B - 1) as b:
                body(h * B + b, h, b, False)
            body(h * B + (B - 1), h, B - 1, True)
        with eng.Fori(0, B - 1) as b:
            body(b + (H - 1) * B, H - 1, b, False)
        body(H * B - 1, H - 1, B - 1, None)

    with nc.Block() as block:
        @block.sync
        def _(sp):
            def load_weights(h):
                for k in range(3):
                    if not isinstance(h, int):
                        sp.wait_ge(w_split[k], h * 2)
                    sp.dma_start(w_raw[k][:], w_dram[k][:, :, bass.ds(h * HD, HD)]).then_inc(w_loaded[k], 16)

            def swap(i, k):
                sp.wait_ge(evacuated[k], i + 1)
                sp.dma_start(s_swap[k][0:64, :], s_full[k][64:128, :]).then_inc(swapped[k], 16)
                sp.dma_start(s_swap[k][64:128, :], s_full[k][0:64, :]).then_inc(swapped[k], 16)

            def body(i, h, b, switch):
                if switch is not None:
                    swap(i + 1, 0)
                    swap(i + 1, 1)
                sp.wait_ge(out_evacuated, i + 2)
                sp.dma_start(o_dram[bass.ds(b, 1), :, bass.ds(h, 1), :].rearrange("a p h n -> p (a h) n"),
                             o_sb[:].rearrange("p (a n) -> p a n", a=1)).then_inc(out_slot_free, 16)

            load_weights(0)
            sp.dma_start(rope[:].rearrange("p a n -> p (a n)"), rope_d).then_inc(rope_loaded, 16)
            swap(0, 0)
            swap(0, 1)
            units(sp, body, lambda h: load_weights(h + 1))
            sp.wait_ge(out_slot_free, 16 + 16 * H * B)

        @block.gpsimd
        def _(pool):
            def split_weights(h):
                for k in range(3):
                    pool.wait_ge(w_split[k], h * 2 + 1)
                    nc.gpsimd.tensor_tensor(w_lo[k][:], w_raw[k][:], f32(w_hi[k][:]), ALU.subtract).then_inc(w_split[k], 1)

            def sines(i):
                for k in range(2):
                    pool.wait_ge(swapped[k], i * 32 + 32)
                    nc.gpsimd.tensor_tensor(s_swap[k][:], s_swap[k][:], rope[:, 2 * k + 1, :], ALU.mult).then_inc(sin_done[k], 1)

            def body(i, h, b, switch):
                if switch:
                    split_weights(h + 1)
                if switch is not None:
                    sines(i + 1)

            nc.gpsimd.memset(o_sb[:], 0.0).then_inc(out_slot_free, 16)
            nc.gpsimd.memset(neg1[:], 0.0).then_inc(out_evacuated, 1)
            split_weights(0)
            pool.wait_ge(rope_loaded, 16)
            sines(0)
            units(pool, body)

        @block.tensor
        def _(pe):
            def project(i, k, batch):
                n = 0
                for c in range(C):
                    for w, v in ((w_hi, xt_hi), (w_hi, xt_lo), (w_lo, xt_hi)):
                        last = nc.tensor.matmul(banks[QB[k]][:, :], w[k][:, c, :], v[:, bass.ds(batch, 1), c, :],
                                                start=(n == 0), stop=(n == 3 * C - 1))
                        n += 1
                last.then_inc(projected[k], 1)

            def project_all(i, h, batch, first=False):
                for k in range(3):
                    pe.wait_ge(w_split[k], h * 2 + 2)
                    if k == 0:
                        pe.wait_ge(out_evacuated, i if not first else 1)
                    if k == 2:
                        pe.wait_ge(evacuated[0], i + 1)
                    project(i, k, batch)

            def body(i, h, b, switch):
                pe.wait_ge(evacuated[2], i + 1)
                for t in range(T):
                    last = nc.tensor.transpose(banks[6][:, t * P:(t + 1) * P], vt[:, t * P:(t + 1) * P], m("ident"))
                last.then_inc(v_transposed, 1)
                pe.wait_ge(lo_done[0], i + 1)
                pe.wait_ge(lo_done[1], i + 1)
                for t in range(T):
                    w = max(256, (t + 1) * P)
                    for n, (a, v) in enumerate(((qk_hi[0], qk_hi[1]), (qk_hi[0], qk_lo[1]), (qk_lo[0], qk_hi[1]))):
                        nc.tensor.matmul(banks[t][:, 0:w], a[:, t * P:(t + 1) * P], v[:, 0:w], start=(n == 0), stop=(n == 2))
                    nc.tensor.matmul(banks[t][:, t * P:(t + 1) * P], ident_b[:], causal_b[:], start=False, stop=True,
                                     skip_group_check=True).then_inc(scores_ready, 1)
                if switch is not None:
                    project_all(i + 1, h + 1 if switch else h, 0 if switch else b + 1)
                pe.wait_ge(v_lo_done, i + 1)
                if switch is not None:
                    pe.wait_ge(evacuated[1], i + 2)
                pe.wait_ge(probs_ready, i * T + T)
                for bank, js in ((6, (0,)), (7, (1,)), (5, (2, 3))):
                    at = 0
                    for j in js:
                        for t in range(j, T):
                            last = nc.tensor.transpose(banks[bank][:, at:at + P],
                                                       e1[:, E1OFF[t] + j * P:E1OFF[t] + (j + 1) * P], m("ident"))
                            at += P
                    last.then_inc(pt_ready, 1)
                if switch is not None:
                    pe.wait_ge(evacuated[2], i + 2)
                n = 0
                for j in range(T):
                    if j < 3:
                        pe.wait_ge(pt_hi_done, i * 3 + j + 1)
                        pe.wait_ge(pt_lo_done, i * 3 + j + 1)
                    w = N - PTQ0[j]
                    for v, p in ((v_hi, pt_hi), (v_hi, pt_lo), (v_lo, pt_hi)):
                        last = nc.tensor.matmul(banks[4][:, PTQ0[j]:N], v[:, j, :], p[:, PTOFF[j]:PTOFF[j] + w],
                                                start=(n == 0), stop=(n == 3 * T - 1), skip_group_check=True)
                        n += 1
                last.then_inc(out_ready, 1)

            pe.wait_ge(zeros_set, 2)
            project_all(0, 0, 0, first=True)
            units(pe, body)

        @block.scalar
        def _(act):
            def evacuate(i, k):
                act.wait_ge(projected[k], i + 1)
                nc.scalar.activation((s_full[0], s_full[1], vt)[k][:], banks[QB[k]][:, :], ACT.Copy)\
                    .then_inc(evacuated[k], 1)

            def split_weights(h):
                for k in range(3):
                    act.wait_ge(w_loaded[k], h * 16 + 16)
                    if not isinstance(h, int):
                        act.wait_ge(projected[k], h * B)
                    nc.scalar.activation(w_hi[k][:], w_raw[k][:], ACT.Copy).then_inc(w_split[k], 1)

            def high(i, k):
                act.wait_ge(roped[k], i + 1)
                nc.scalar.activation(qk_hi[k][:], s_full[k][:], ACT.Copy).then_inc(hi_done[k], 1)

            def body(i, h, b, switch):
                if switch:
                    split_weights(h + 1)
                act.wait_ge(v_transposed, i + 1)
                nc.scalar.activation(v_hi[:].rearrange("p t d -> p (t d)"), banks[6][:, :], ACT.Copy).then_inc(v_hi_done, 1)
                for t in range(T):
                    w = (t + 1) * P
                    act.wait_ge(negmax, i * T + t + 1)
                    nc.scalar.activation(e1[:, E1OFF[t]:E1OFF[t] + w], banks[t][:, 0:w], ACT.Exp, bias=neg1[:, t:t + 1],
                                         accum_out=sums[:, 1, t:t + 1]).then_inc(exp_full, 1)
                if switch is not None:
                    evacuate(i + 1, 0)
                act.wait_ge(negmax2, i + 1)
                for t in range(T):
                    lo = WIN if t == 0 else 0
                    nc.scalar.activation(e2[:, t, lo:], e2[:, t, lo:], ACT.Exp, bias=neg2[:, t:t + 1],
                                         accum_out=sums[:, 2, t:t + 1]).then_inc(exp_win, 1)
                act.wait_ge(cmp_step, i * NC + T + 3)
                nc.scalar.activation(sc[:], sc2[:], ACT.Exp).then_inc(exp_cmp, 1)
                if switch is not None:
                    evacuate(i + 1, 1)
                    evacuate(i + 1, 2)
                    high(i + 1, 0)
                for g in range(3):
                    w = (512, 384, 384)[g]
                    act.wait_ge(pt_ready, i * 3 + g + 1)
                    if g < 2:
                        nc.scalar.activation(pt_hi[:, PTOFF[g]:PTOFF[g] + w], banks[6 + g][:, 0:w], ACT.Copy).then_inc(pt_hi_done, 1)
                    else:
                        nc.scalar.activation(pt_hi[:, PTOFF[2]:PTOFF[2] + 256], banks[5][:, 0:256], ACT.Copy)
                        nc.scalar.activation(pt_hi[:, PTW - P:PTW], banks[5][:, 256:384], ACT.Copy).then_inc(pt_hi_done, 1)
                if switch is not None:
                    high(i + 1, 1)
                act.wait_ge(out_ready, i + 1)
                act.wait_ge(out_slot_free, i * 16 + 16)
                nc.scalar.activation(o_sb[:], banks[4][:, :], ACT.Copy).then_inc(out_evacuated, 1)

            split_weights(0)
            for k in range(3):
                evacuate(0, k)
            for k in range(2):
                high(0, k)
            units(act, body)

        @block.vector
        def _(dve):
            def cosines(i, k):
                dve.wait_ge(swapped[k], i * 32 + 32)
                nc.vector.tensor_tensor(s_full[k][:], s_full[k][:], rope[:, 2 * k, :], ALU.mult).then_inc(cos_done[k], 1)

            def rotate(i, k):
                dve.wait_ge(cos_done[k], i + 1)
                dve.wait_ge(sin_done[k], i + 1)
                nc.vector.tensor_tensor(s_full[k][:], s_full[k][:], s_swap[k][:], ALU.add).then_inc(roped[k], 1)

            def low(i, k):
                dve.wait_ge(hi_done[k], i + 1)
                nc.vector.tensor_tensor(qk_lo[k][:], s_full[k][:], f32(qk_hi[k][:]), ALU.subtract).then_inc(lo_done[k], 1)

            def body(i, h, b, switch):
                dve.wait_ge(v_hi_done, i + 1)
                nc.vector.tensor_tensor(v_lo[:].rearrange("p t d -> p (t d)"), banks[6][:, :],
                                        f32(v_hi[:].rearrange("p t d -> p (t d)")), ALU.subtract).then_inc(v_lo_done, 1)
                for t in range(T):
                    w = (t + 1) * P
                    dve.wait_ge(scores_ready, i * T + t + 1)
                    nc.vector.reduce_max(neg1[:, t:t + 1], banks[t][:, 0:w], AX.X, negate=True).then_inc(negmax, 1)
                for t in range(T):
                    nb = 2 * (t + 1)
                    dve.wait_ge(exp_full, i * T + t + 1)
                    nc.vector.reduce_sum(sc[:, t, 0:nb], banks[t][:, 0:nb * BS].rearrange("p (n s) -> p n s", s=BS),
                                         AX.X).then_inc(cmp_step, 1)
                    lo = WIN if t == 0 else 0
                    k0 = t * P - WIN + lo
                    nc.vector.tensor_tensor_reduce(out=e2[:, t, lo:], in0=banks[t][:, k0:(t + 1) * P],
                                                   in1=m("window")[:, lo:], scale=1.0, scalar=-3e38, op0=ALU.add, op1=ALU.max,
                                                   accum_out=max2[:, t:t + 1]).then_inc(window_masked, 1)
                dve.wait_ge(window_masked, i * T + T)
                nc.vector.tensor_scalar(neg2[:], max2[:], -1.0, None, ALU.mult).then_inc(negmax2, 1)
                dve.wait_ge(cmp_step, i * NC + T)
                nc.vector.scalar_tensor_tensor(out=sc2[:], in0=sc[:], scalar=1.0 / BS,
                                               in1=m("cmask").rearrange("p (t n) -> p t n", n=NB),
                                               op0=ALU.mult, op1=ALU.add).then_inc(cmp_step, 1)
                dve.wait_ge(cmp_step, i * NC + T + 1)
                nc.vector.reduce_max(mc[:], sc2[:], AX.X).then_inc(cmp_step, 1)
                dve.wait_ge(cmp_step, i * NC + T + 2)
                nc.vector.tensor_tensor(sc2[:], sc2[:], mc[:].rearrange("p (t o) -> p t o", o=1).to_broadcast([P, T, NB]),
                                        ALU.subtract).then_inc(cmp_step, 1)
                if switch is not None:
                    cosines(i + 1, 0)
                    rotate(i + 1, 0)
                dve.wait_ge(exp_cmp, i + 1)
                nc.vector.reduce_sum(sums[:, 0, :], sc[:], AX.X).then_inc(cmp_step, 1)
                dve.wait_ge(exp_win, i * T + T)
                dve.wait_ge(cmp_step, i * NC + T + 4)
                nc.vector.reciprocal(coef[:], sums[:]).then_inc(cmp_step, 1)
                dve.wait_ge(cmp_step, i * NC + T + 5)
                nc.vector.tensor_tensor(coef[:].rearrange("p (o r) t -> p o r t", o=1), coef[:].rearrange("p (o r) t -> p o r t", o=1),
                                        gates[:, bass.ds(b, 1), bass.ds(h, 1)].rearrange("p a h r t -> p (a h) r t"),
                                        ALU.mult).then_inc(cmp_step, 1)
                dve.wait_ge(cmp_step, i * NC + T + 6)
                nc.vector.tensor_tensor(cb[:], sc[:], coef[:, 0, :].rearrange("p (t o) -> p t o", o=1).to_broadcast([P, T, NB]),
                                        ALU.mult).then_inc(cmp_step, 1)
                dve.wait_ge(cmp_step, i * NC + T + 7)
                for t in range(T):
                    nb = 2 * (t + 1)
                    e = e1[:, E1OFF[t]:E1OFF[t] + nb * BS].rearrange("p (n s) -> p n s", s=BS)
                    nc.vector.scalar_tensor_tensor(out=e, in0=e, scalar=coef[:, 1, t:t + 1],
                                                   in1=cb[:, t, 0:nb].rearrange("p (n o) -> p n o", o=1).to_broadcast([P, nb, BS]),
                                                   op0=ALU.mult, op1=ALU.add).then_inc(mixed, 1)
                for t in range(T):
                    lo = WIN if t == 0 else 0
                    k0 = t * P - WIN + lo
                    dve.wait_ge(mixed, i * T + t + 1)
                    e = e1[:, E1OFF[t] + k0:E1OFF[t] + (t + 1) * P]
                    nc.vector.scalar_tensor_tensor(out=e, in0=e2[:, t, lo:], scalar=coef[:, 2, t:t + 1], in1=e,
                                                   op0=ALU.mult, op1=ALU.add).then_inc(probs_ready, 1)
                if switch is not None:
                    low(i + 1, 0)
                    cosines(i + 1, 1)
                    rotate(i + 1, 1)
                for g in range(3):
                    w = (512, 384, 384)[g]
                    dve.wait_ge(pt_hi_done, i * 3 + g + 1)
                    if g < 2:
                        nc.vector.tensor_tensor(pt_lo[:, PTOFF[g]:PTOFF[g] + w], banks[6 + g][:, 0:w],
                                                f32(pt_hi[:, PTOFF[g]:PTOFF[g] + w]), ALU.subtract).then_inc(pt_lo_done, 1)
                    else:
                        nc.vector.tensor_tensor(pt_lo[:, PTOFF[2]:PTOFF[2] + 256], banks[5][:, 0:256],
                                                f32(pt_hi[:, PTOFF[2]:PTOFF[2] + 256]), ALU.subtract)
                        nc.vector.tensor_tensor(pt_lo[:, PTW - P:PTW], banks[5][:, 256:384],
                                                f32(pt_hi[:, PTW - P:PTW]), ALU.subtract).then_inc(pt_lo_done, 1)
                if switch is not None:
                    low(i + 1, 1)

            nc.vector.memset(f32(pt_hi[:, PTOFF[3]:PTOFF[3] + P]), 0.0).then_inc(zeros_set, 1)
            nc.vector.memset(f32(pt_lo[:, PTOFF[3]:PTOFF[3] + P]), 0.0).then_inc(zeros_set, 1)
            nc.vector.memset(sc[:], 0.0).then_inc(zeros_set, 1)
            dve.wait_ge(zeros_set, 3)
            dve.wait_ge(rope_loaded, 16)
            for k in range(2):
                cosines(0, k)
                rotate(0, k)
                low(0, k)
            units(dve, body)


def feed_forward(nc, misc_end, banks, m, o_dram, x, wo, wr, br, w1, b1, w2, b2, out):
    r = Region(nc, misc_end)
    zsel_hi = r("zsel_hi", [P, C, B * P], F32R)
    zsel_lo = r("zsel_lo", [P, C, B * P], F32R)
    place = r("place", [P, B, N], F32R)
    weight = r("weight", [P, B, T])
    base_dram = nc.dram_tensor("base_scratch", [B, P, T, D], F32, kind="Internal").ap()
    project_and_route(nc, r.at, banks, m, o_dram, x, wo, wr, br, zsel_hi, zsel_lo, place, weight, base_dram)
    experts(nc, r.at, banks, zsel_hi, zsel_lo, place, weight, base_dram, w1, b1, w2, b2, out)


def project_and_route(nc, at, banks, m, o_dram, x, wo, wr, br, zsel_hi, zsel_lo, place, weight, base_dram):
    r = Region(nc, at)
    G = 4
    K = H // G
    wo_hi, wo_lo = r("wo_hi", [P, H, D], F32R), r("wo_lo", [P, H, D], F32R)
    o_raw = [r(f"o_raw{s}", [P, G, N]) for s in range(2)]
    o_hi = [r(f"o_hi{s}", [P, G, N], F32R) for s in range(2)]
    o_lo = [r(f"o_lo{s}", [P, G, N], F32R) for s in range(2)]
    xin = r("xin2", [P, T, D])
    x1 = r("x1", [P, T, D])
    z2 = r("z2", [P, T, D])
    wr_all = r("wr_all", [P, D])
    junk = r("junk", [P, D])
    diag = r("diag", [P, N])
    onehot = r("onehot", [P, T, P])
    br_all = r("br_all", [P, 1])
    stats, mv = r("stats2", [P, T, 6]), r("mv2", [P, T, 2])
    ve, sd, y, yy = (r(f"{k}_2", [P, T]) for k in ("ve", "sd", "y", "yy"))
    wraw, wcol, count, sel, unsel, selcum, slot_sb = (r(k, [P, T]) for k in ("wraw", "wcol", "count", "sel", "unsel", "selcum", "slot_sb"))
    assert r.at <= nc.sbuf_usable_end, r.at
    wo_v = wo.rearrange("(k g p) d -> k p g d", p=P, g=G)

    S = nc.alloc_semaphore
    small_loaded = S("small_loaded")
    raw_loaded = [S("raw_loaded0"), S("raw_loaded1")]
    hi_split, lo_split, chunk_used = S("hi_split"), S("lo_split"), S("chunk_used")
    x_loaded, acc_ready, x1_ready = S("x2_loaded"), S("acc_ready"), S("x1_ready")
    step, sd_ready, z2_ready = S("route_step"), S("sd2_ready"), S("z2_ready")
    diag_ready, row_ready, sel_ready, slot_ready = S("diag_ready"), S("row_ready"), S("sel_ready"), S("slot_ready")
    onehot_ready, zsel_ready, place_ready = S("onehot_ready"), S("zsel_ready"), S("place_ready")
    zsel_hi_done, zsel_lo_done, place_done = S("zsel_hi_done"), S("zsel_lo_done"), S("place_done")
    base_ready, base_stored = S("base_ready"), S("base_stored")
    NS = 4 + 4 + 1 + 5 + T + 1 + 1 + T + 1 + 3 + 1

    def batches(eng, body):
        with eng.Fori(0, B - 1) as b:
            body(b, True)
        body(B - 1, False)

    with nc.Block() as block:
        @block.sync
        def _(sp):
            def load_o(b, k):
                sp.wait_ge(lo_split, b * K + K + k - 1)
                sp.dma_start(o_raw[k % 2][:], o_dram[bass.ds(b, 1), :, k * G:(k + 1) * G, :].rearrange("o p g n -> p (o g) n"))\
                    .then_inc(raw_loaded[k % 2], 16)

            def load_x(b):
                sp.wait_ge(x1_ready, b * T + 1)
                sp.dma_start(xin[:], x[bass.ds(b, 1)].rearrange("o (t p) d -> p (o t) d", p=P)).then_inc(x_loaded, 16)

            def body(b, more):
                if more:
                    for k in range(K):
                        load_o(b + 1, k)
                        if k == 1:
                            load_x(b + 1)
                sp.wait_ge(base_ready, b * T + T)
                sp.dma_start(base_dram[bass.ds(b, 1)].rearrange("o p t d -> p (o t) d"), x1[:]).then_inc(base_stored, 16)

            for k in range(K):
                if k >= 2:
                    sp.wait_ge(lo_split, k - 1)
                sp.dma_start(o_raw[k % 2][:], wo_v[k]).then_inc(raw_loaded[k % 2], 16)
            sp.dma_start(wr_all[:], wr.rearrange("d o -> o d").to_broadcast([P, D])).then_inc(small_loaded, 16)
            sp.dma_start(br_all[:], br.rearrange("(o d) -> o d", o=1).to_broadcast([P, 1])).then_inc(small_loaded, 16)
            for k in range(K):
                load_o(0, k)
            load_x(0)
            batches(sp, body)
            sp.wait_ge(base_stored, 16 + 16 * B)

        @block.scalar
        def _(act):
            def high(b, k):
                act.wait_ge(raw_loaded[k % 2], b * 32 + (k // 2) * 16 + 48)
                act.wait_ge(chunk_used, b * K + k + 1)
                nc.scalar.activation(o_hi[k % 2][:], o_raw[k % 2][:], ACT.Copy).then_inc(hi_split, 1)

            def body(b, more):
                if more:
                    high(b + 1, 0)
                    high(b + 1, 1)
                act.wait_ge(step, b * NS + 9)
                nc.scalar.activation(sd[:], ve[:], ACT.Sqrt).then_inc(sd_ready, 1)
                if more:
                    high(b + 1, 2)
                    high(b + 1, 3)
                act.wait_ge(zsel_ready, b + 1)
                nc.scalar.activation(zsel_hi[:, :, bass.ds(b * P, P)], banks[6][:, :].rearrange("p (c s) -> p c s", c=C),
                                     ACT.Copy).then_inc(zsel_hi_done, 1)
                act.wait_ge(place_ready, b + 1)
                nc.scalar.activation(place[:, bass.ds(b, 1), :], banks[7][:, :], ACT.Copy).then_inc(place_done, 1)

            for k in range(K):
                act.wait_ge(raw_loaded[k % 2], k // 2 * 16 + 16)
                nc.scalar.activation(wo_hi[:, k * G:(k + 1) * G, :], o_raw[k % 2][:], ACT.Copy).then_inc(hi_split, 1)
            for k in range(K):
                high(0, k)
            batches(act, body)

        @block.gpsimd
        def _(pool):
            def low(b, k):
                pool.wait_ge(hi_split, b * K + K + k + 1)
                nc.gpsimd.tensor_tensor(o_lo[k % 2][:], o_raw[k % 2][:], f32(o_hi[k % 2][:]), ALU.subtract).then_inc(lo_split, 1)

            nc.gpsimd.memset(y[:], 0.0).then_inc(chunk_used, 1)
            nc.gpsimd.memset(yy[:], 0.0).then_inc(chunk_used, 1)
            nc.gpsimd.memset(sd[:], 0.0).then_inc(x1_ready, 1)
            nc.gpsimd.memset(ve[:], 0.0).then_inc(base_stored, 16)
            for k in range(K):
                pool.wait_ge(hi_split, k + 1)
                nc.gpsimd.tensor_tensor(wo_lo[:, k * G:(k + 1) * G, :], o_raw[k % 2][:], f32(wo_hi[:, k * G:(k + 1) * G, :]),
                                        ALU.subtract).then_inc(lo_split, 1)
            for k in range(K):
                low(0, k)
            with pool.Fori(0, B - 1) as b:
                for k in range(K):
                    low(b + 1, k)

        @block.tensor
        def _(pe):
            def chunk(b, k, first=False):
                pe.wait_ge(lo_split, b * K + K + k + 1)
                for t in range(T):
                    if k == 0 and not first:
                        pe.wait_ge(x1_ready, b * T + (t - 2))
                    n = 0
                    for g in range(G):
                        for o, w in ((o_hi, wo_hi), (o_hi, wo_lo), (o_lo, wo_hi)):
                            last = nc.tensor.matmul(banks[t][:, :], o[k % 2][:, g, t * P:(t + 1) * P], w[:, k * G + g, :],
                                                    start=(k == 0 and n == 0), stop=(k == K - 1 and n == 3 * G - 1))
                            n += 1
                    if k == K - 1 and t < T - 1:
                        last.then_inc(acc_ready, 1)
                last.then_inc(chunk_used, 1)

            def body(b, more):
                if more:
                    chunk(b + 1, 0)
                pe.wait_ge(diag_ready, b * T + T)
                nc.tensor.matmul(banks[4][:, :], m("ones"), diag[:], start=True, stop=True).then_inc(row_ready, 1)
                if more:
                    chunk(b + 1, 1)
                pe.wait_ge(sel_ready, b + 1)
                nc.tensor.matmul(banks[5][:, 0:T], m("before"), sel[:], start=True, stop=False)
                nc.tensor.matmul(banks[5][:, 0:T], m("ones"), selcum[:], start=False, stop=True).then_inc(slot_ready, 1)
                if more:
                    chunk(b + 1, 2)
                pe.wait_ge(onehot_ready, b * T + T)
                for c in range(C):
                    for t in range(T):
                        last = nc.tensor.matmul(banks[6][:, c * P:(c + 1) * P], z2[:, t, c * P:(c + 1) * P], onehot[:, t, :],
                                                start=(t == 0), stop=(t == T - 1))
                last.then_inc(zsel_ready, 1)
                for t in range(T):
                    last = nc.tensor.transpose(banks[7][:, t * P:(t + 1) * P], onehot[:, t, :], m("ident"))
                last.then_inc(place_ready, 1)
                if more:
                    chunk(b + 1, 3)

            for k in range(K):
                chunk(0, k, first=True)
            batches(pe, body)

        @block.vector
        def _(dve):
            v = nc.vector

            def body(b, more):
                at = [0]

                def after():
                    dve.wait_ge(step, b * NS + at[0])

                def did(ins):
                    ins.then_inc(step, 1)
                    at[0] += 1

                dve.wait_ge(x_loaded, b * 16 + 16)
                dve.wait_ge(base_stored, b * 16 + 16)
                for t in range(T):
                    if t < T - 1:
                        dve.wait_ge(acc_ready, b * (T - 1) + t + 1)
                    else:
                        dve.wait_ge(chunk_used, b * K + K + 2)
                    v.tensor_tensor(x1[:, t], xin[:, t], banks[t][:, :], ALU.add).then_inc(x1_ready, 1)
                for t in range(T):
                    dve.wait_ge(x1_ready, b * T + t + 2)
                    did(v.bn_stats(stats[:, t], x1[:, t]))
                after()
                v.memset(yy[:], 0.0)
                for t in range(T):
                    did(v.bn_aggr(mv[:, t], stats[:, t]))
                after()
                did(v.tensor_scalar(ve[:], mv[:, :, 1], EPS, None, ALU.add))
                dve.wait_ge(sd_ready, b + 1)
                did(v.reciprocal(y[:], sd[:]))
                after()
                did(v.tensor_tensor(yy[:], y[:], y[:], ALU.mult))
                after()
                did(v.tensor_tensor(yy[:], yy[:], ve[:], ALU.mult))
                after()
                did(v.tensor_scalar(yy[:], yy[:], -0.5, 1.5, ALU.mult, ALU.add))
                after()
                did(v.tensor_tensor(y[:], yy[:], y[:], ALU.mult))
                after()
                for t in range(T):
                    v.tensor_scalar(z2[:, t], x1[:, t], mv[:, t, 0:1], y[:, t:t + 1], ALU.subtract, ALU.mult).then_inc(z2_ready, 1)
                dve.wait_ge(small_loaded, 32)
                for t in range(T):
                    dve.wait_ge(z2_ready, b * T + t + 1)
                    after()
                    did(v.tensor_tensor_reduce(out=junk[:], in0=z2[:, t], in1=wr_all[:], scale=1.0, scalar=0.0,
                                               op0=ALU.mult, op1=ALU.add, accum_out=wraw[:, t:t + 1]))
                after()
                did(v.tensor_scalar(wcol[:], wraw[:], br_all[:, 0:1], None, ALU.add))
                did(v.tensor_scalar(weight[:, bass.ds(b, 1), :], wraw[:].rearrange("p (o t) -> p o t", o=1), br_all[:, 0:1], None, ALU.add))
                after()
                for t in range(T):
                    v.tensor_scalar(diag[:, t * P:(t + 1) * P], m("ident"), wcol[:, t:t + 1], None, ALU.mult).then_inc(diag_ready, 1)
                dve.wait_ge(row_ready, b + 1)
                for t in range(T):
                    after()
                    did(v.tensor_scalar(junk[:], banks[4][:, :], wcol[:, t:t + 1], None, ALU.is_ge, ALU.add,
                                        accum_out=count[:, t:t + 1]))
                after()
                did(v.tensor_scalar(sel[:], count[:], float(KTOP), None, ALU.is_lt))
                after()
                did(v.tensor_copy(selcum[:, 1:2], sel[:, 0:1]))
                v.tensor_scalar(unsel[:], sel[:], -1.0, 1.0, ALU.mult, ALU.add).then_inc(step, 1)
                at[0] += 1
                after()
                did(v.tensor_tensor(selcum[:, 2:3], selcum[:, 1:2], sel[:, 1:2], ALU.add))
                after()
                v.tensor_tensor(selcum[:, 3:4], selcum[:, 2:3], sel[:, 2:3], ALU.add).then_inc(sel_ready, 1)
                for t in range(T):
                    v.scalar_tensor_tensor(out=x1[:, t], in0=z2[:, t], scalar=unsel[:, t:t + 1], in1=x1[:, t],
                                           op0=ALU.mult, op1=ALU.add).then_inc(base_ready, 1)
                dve.wait_ge(slot_ready, b + 1)
                did(v.tensor_copy(slot_sb[:], banks[5][:, 0:T]))
                after()
                for t in range(T):
                    v.tensor_scalar(onehot[:, t], m("slot"), slot_sb[:, t:t + 1], sel[:, t:t + 1],
                                    ALU.is_equal, ALU.mult).then_inc(onehot_ready, 1)
                dve.wait_ge(zsel_hi_done, b + 1)
                v.tensor_tensor(zsel_lo[:, :, bass.ds(b * P, P)], banks[6][:, :].rearrange("p (c s) -> p c s", c=C),
                                f32(zsel_hi[:, :, bass.ds(b * P, P)]), ALU.subtract).then_inc(zsel_lo_done, 1)
                assert at[0] == NS, (at[0], NS)

            v.memset(selcum[:], 0.0)
            batches(dve, body)


def experts(nc, at, banks, zsel_hi, zsel_lo, place, weight, base_dram, w1, b1, w2, b2, out):
    r = Region(nc, at)
    GB = 4
    NG = B // GB
    w1_raw, w2_raw = ([r(f"{n}{s}", [P, 512]) for s in range(2)] for n in ("w1_raw", "w2_raw"))
    w1_hi, w1_lo, w2_hi, w2_lo = ([r(f"{n}{s}", [P, 512], F32R) for s in range(2)] for n in ("w1_hi", "w1_lo", "w2_hi", "w2_lo"))
    b1_sb = r("b1_sb", [P, FT])
    b2_all = r("b2_all", [P, D])
    hid = [r(f"hid{s}", [P, GB * P]) for s in range(2)]
    hid_hi = [r(f"hid_hi{s}", [P, GB * P], F32R) for s in range(2)]
    hid_lo = [r(f"hid_lo{s}", [P, GB * P], F32R) for s in range(2)]
    ff = r("ff", [P, GB, D])
    ff_hi, ff_lo = r("ff_hi", [P, GB, D], F32R), r("ff_lo", [P, GB, D], F32R)
    base = [r(f"base{s}", [P, T, D]) for s in range(2)]
    assert r.at <= nc.sbuf_usable_end, r.at
    w1_v = w1.rearrange("(c p) f -> p c f", p=P)
    w2_v = w2.rearrange("(f p) d -> f p d", p=P)

    S = nc.alloc_semaphore
    bias_loaded = S("bias_loaded")
    w_loaded = [S("w12_loaded0"), S("w12_loaded1")]
    w1_hi_done, w1_lo_done, w2_hi_done, w2_lo_done = S("w1_hi_done"), S("w1_lo_done"), S("w2_hi_done"), S("w2_lo_done")
    hid_ready, gelu_done, hid_hi_done, hid_lo_done = S("hid_ready"), S("gelu_done"), S("hid_hi_done"), S("hid_lo_done")
    step_done, ffacc_ready, ff_ready = S("step_done"), S("ffacc_ready"), S("ff_ready")
    ff_hi_done, ff_lo_done = S("ff_hi_done"), S("ff_lo_done")
    spread_ready, final_ready, stored = S("spread_ready"), S("final_ready"), S("stored")
    base_loaded = [S("base_loaded0"), S("base_loaded1")]

    def tiles(eng, g, body):
        at = g * FT // 2
        for s in range(2):
            body(at, s, s, s == 0, False)
        with eng.Fori(1, FT // 2 - 1) as pair:
            for s in range(2):
                body(pair + at, s, pair * 2 + s, False, False)
        for s in range(2):
            body(at + FT // 2 - 1, s, FT - 2 + s, False, s == 1)

    with nc.Block() as block:
        @block.sync
        def _(sp):
            def load(pair, s, f, first, last):
                if isinstance(pair, int) and pair and pair % (FT // 2) == 0 and not last:
                    return
                load_ahead(pair, s, f)

            def load_ahead(pair, s, f):
                if not (isinstance(pair, int) and pair == 0):
                    sp.wait_ge(w1_lo_done, pair * 2 + s - 1)
                    sp.wait_ge(w2_lo_done, pair * 2 + s - 1)
                sp.dma_start(w1_raw[s][:].rearrange("p (c f) -> p c f", c=C), w1_v[:, :, bass.ds(f * P, P)]).then_inc(w_loaded[s], 16)
                sp.dma_start(w2_raw[s][:], w2_v[bass.ds(f, 1)].rearrange("o p d -> p (o d)")).then_inc(w_loaded[s], 16)

            def load_base(b):
                if b >= 2:
                    sp.wait_ge(stored, 16 * (b - 1))
                sp.dma_start(base[b % 2][:], base_dram[b]).then_inc(base_loaded[b % 2], 16)

            sp.dma_start(b1_sb[:], b1).then_inc(bias_loaded, 16)
            sp.dma_start(b2_all[:], b2.rearrange("(o d) -> o d", o=1).to_broadcast([P, D])).then_inc(bias_loaded, 16)
            load_base(0)
            load_base(1)
            for g in range(NG):
                tiles(sp, g, load)
                if g + 1 < NG:
                    for s in range(2):
                        load_ahead((g + 1) * FT // 2, s, s)
                for b in range(g * GB, (g + 1) * GB):
                    sp.wait_ge(final_ready, (b + 1) * T)
                    sp.dma_start(out[b].rearrange("(t p) d -> p t d", p=P), base[b % 2][:]).then_inc(stored, 16)
                    if b + 2 < B:
                        load_base(b + 2)
            sp.wait_ge(stored, 16 * B)

        @block.gpsimd
        def _(pool):
            def low(pair, s, f, first, last):
                for raw, hi, lo, hi_done, lo_done in ((w1_raw, w1_hi, w1_lo, w1_hi_done, w1_lo_done),
                                                      (w2_raw, w2_hi, w2_lo, w2_hi_done, w2_lo_done)):
                    pool.wait_ge(hi_done, pair * 2 + s + 1)
                    nc.gpsimd.tensor_tensor(lo[s][:], raw[s][:], f32(hi[s][:]), ALU.subtract).then_inc(lo_done, 1)

            for g in range(NG):
                tiles(pool, g, low)

        @block.scalar
        def _(act):
            def high(which, pair, s):
                raw, hi, done = ((w1_raw, w1_hi, w1_hi_done), (w2_raw, w2_hi, w2_hi_done))[which]
                act.wait_ge(w_loaded[s], pair * 32 + 32)
                if not (isinstance(pair, int) and pair == 0):
                    act.wait_ge((hid_ready, step_done)[which], pair * 2 + s - 1)
                nc.scalar.activation(hi[s][:], raw[s][:], ACT.Copy).then_inc(done, 1)

            def body(pair, s, f, first, last):
                nxt = (pair + s, 1 - s)
                end = last and pair == B * P * FT // (GB * P) // 2 - 1
                if not end:
                    high(0, *nxt)
                act.wait_ge(hid_ready, pair * 2 + s + 1)
                nc.scalar.activation(hid[s][:], banks[4 + s][:, :], ACT.Gelu_apprx_tanh, bias=b1_sb[:, bass.ds(f, 1)]).then_inc(gelu_done, 1)
                act.wait_ge(gelu_done, pair * 2 + s + 1)
                nc.scalar.activation(hid_hi[s][:], hid[s][:], ACT.Copy).then_inc(hid_hi_done, 1)
                if not end:
                    high(1, *nxt)

            act.wait_ge(bias_loaded, 32)
            high(0, 0, 0)
            high(1, 0, 0)
            for g in range(NG):
                tiles(act, g, body)
                for q in range(GB):
                    act.wait_ge(ff_ready, g * GB + q + 1)
                    nc.scalar.activation(ff_hi[:, q], ff[:, q], ACT.Copy).then_inc(ff_hi_done, 1)

        @block.tensor
        def _(pe):
            def hidden(g, pair, s):
                pe.wait_ge(w1_lo_done, pair * 2 + s + 1)
                k = 0
                for c in range(C):
                    for w, z in ((w1_hi, zsel_hi), (w1_hi, zsel_lo), (w1_lo, zsel_hi)):
                        last = nc.tensor.matmul(banks[4 + s][:, :], w[s][:, c * P:(c + 1) * P], z[:, c, g * GB * P:(g + 1) * GB * P],
                                                start=(k == 0), stop=(k == 3 * C - 1))
                        k += 1
                last.then_inc(hid_ready, 1)

            for g in range(NG):
                def body(pair, s, f, first, last):
                    if not last:
                        hidden(g, pair + s, 1 - s)
                    pe.wait_ge(w2_lo_done, pair * 2 + s + 1)
                    pe.wait_ge(hid_lo_done, pair * 2 + s + 1)
                    for q in range(GB):
                        for k, (h, w) in enumerate(((hid_hi, w2_hi), (hid_hi, w2_lo), (hid_lo, w2_hi))):
                            ins = nc.tensor.matmul(banks[q][:, :], h[s][:, q * P:(q + 1) * P], w[s][:],
                                                   start=(first and k == 0), stop=(last and k == 2))
                        if last and q < GB - 1:
                            ins.then_inc(ffacc_ready, 1)
                    ins.then_inc(step_done, 1)

                if g:
                    pe.wait_ge(ff_ready, g * GB)
                    pe.wait_ge(final_ready, g * GB * T)
                hidden(g, g * FT // 2, 0)
                tiles(pe, g, body)
                for q in range(GB):
                    b = g * GB + q
                    pe.wait_ge(ff_lo_done, b + 1)
                    for t in range(T):
                        if q:
                            pe.wait_ge(final_ready, (b - 1) * T + t + 1)
                        for k, v in enumerate((ff_hi, ff_lo)):
                            last = nc.tensor.matmul(banks[4 + t][:, :], place[:, b, t * P:(t + 1) * P], v[:, q],
                                                    start=(k == 0), stop=(k == 1))
                        last.then_inc(spread_ready, 1)

        @block.vector
        def _(dve):
            def low(pair, s, f, first, last):
                dve.wait_ge(hid_hi_done, pair * 2 + s + 1)
                nc.vector.tensor_tensor(hid_lo[s][:], hid[s][:], f32(hid_hi[s][:]), ALU.subtract).then_inc(hid_lo_done, 1)

            dve.wait_ge(bias_loaded, 32)
            for g in range(NG):
                tiles(dve, g, low)
                for q in range(GB):
                    if q < GB - 1:
                        dve.wait_ge(ffacc_ready, g * (GB - 1) + q + 1)
                    else:
                        dve.wait_ge(step_done, (g + 1) * FT)
                    nc.vector.tensor_tensor(ff[:, q], banks[q][:, :], b2_all[:], ALU.add).then_inc(ff_ready, 1)
                for q in range(GB):
                    dve.wait_ge(ff_hi_done, g * GB + q + 1)
                    nc.vector.tensor_tensor(ff_lo[:, q], ff[:, q], f32(ff_hi[:, q]), ALU.subtract).then_inc(ff_lo_done, 1)
                for q in range(GB):
                    b = g * GB + q
                    dve.wait_ge(base_loaded[b % 2], 16 * (b // 2 + 1))
                    for t in range(T):
                        dve.wait_ge(spread_ready, b * T + t + 1)
                        nc.vector.scalar_tensor_tensor(out=base[b % 2][:, t], in0=banks[4 + t][:, :], scalar=weight[:, b, t:t + 1],
                                                       in1=base[b % 2][:, t], op0=ALU.mult, op1=ALU.add).then_inc(final_ready, 1)


_INS = ["L0_attn_x", "L0_attn_Wq", "L0_attn_Wk", "L0_attn_Wv", "L0_attn_Wg", "L0_attn_Wo", "L0_ffn_W_r", "L0_ffn_b_r",
        "L0_ffn_W1", "L0_ffn_b1", "L0_ffn_W2", "L0_ffn_b2"]


def given(inputs):
    a = {n: np.ascontiguousarray(inputs[n]) for n in _INS}
    a["L0_ffn_b1"] = np.ascontiguousarray(a["L0_ffn_b1"].reshape(FT, P).T)
    a["rope"], a["misc"] = consts()
    return a


def kernel(**inputs):
    import concourse.bacc as bacc
    from concourse.bass_utils import run_bass_kernel_spmd

    nc = bacc.Bacc("TRN2", target_bir_lowering=False, num_devices=1)
    arrays, args = {}, []
    for name, a in given(inputs).items():
        arrays[f"in_{name}"] = a
        args.append(nc.dram_tensor(f"in_{name}", a.shape, mybir.dt.from_np(a.dtype), kind="ExternalInput").ap())
    out = nc.dram_tensor("out", (B, N, D), F32, kind="ExternalOutput").ap()
    build(nc, *args, out)
    r = run_bass_kernel_spmd(nc, [arrays], core_ids=[0])
    return r.results[0]["out"]
```

```python
import numpy as np
import concourse.bass as bass
from concourse import mybir
from concourse.alu_op_type import AluOpType as ALU

B, N, D = 8, 512, 512
H, HD = 16, 128
BS = 64
NB = N // BS
WIN = 64
DFF = 4 * 512
KTOP = int(0.125 * 1024)
EPS = 1e-5
NEG = -1e30
P = 128
T = N // P
C = D // P
FT = DFF // P
BASE = 10000.0

F32, F32R, BF16 = mybir.dt.float32, mybir.dt.float32r, mybir.dt.bfloat16
ACT = mybir.ActivationFunctionType
AX = mybir.AxisListType

E1OFF = [0, 128, 384, 768]
E1W = 1280
PTOFF = [0, 512, 896, 1152]
PTQ0 = [0, 128, 256, 256]
PTW = 1408


def consts():
    half = HD // 2
    inv = (np.float32(1.0) / np.float32(BASE) ** (np.arange(half, dtype=np.float32) / np.float32(half))).astype(np.float32)
    th = (np.arange(N, dtype=np.float32)[:, None] * inv[None, :]).astype(np.float32)
    cos, sin = np.cos(th).T.astype(np.float32), np.sin(th).T.astype(np.float32)
    cosk = np.concatenate([cos, cos])
    sink = np.concatenate([-sin, sin])
    rope = np.stack([cosk, sink], 1)
    p = np.arange(P)
    ident = np.eye(P)
    causal = np.where(p[None, :] <= p[:, None], 0.0, NEG)
    c = np.arange(P + WIN)
    window = np.where((c[None, :] <= p[:, None] + WIN) & (c[None, :] >= p[:, None]), 0.0, NEG)
    q = p[:, None] + P * np.arange(T)[None, :]
    ends = (np.arange(NB) + 1) * BS - 1
    cmask = np.where(q[:, :, None] >= ends, 0.0, NEG)
    some = (q >= ends[0]) / BS
    before = np.where(p[:, None] < p[None, :], 1.0, 0.0)
    slot = np.broadcast_to(p[None, :], (P, P))
    ones = np.ones((P, P))
    misc = np.concatenate([x.reshape(P, -1) for x in (ident, causal, window, cmask, some)], 1)
    late = np.concatenate([before, slot, ones], 1)
    return rope.reshape(P, -1).astype(np.float32), misc.astype(np.float32), late.astype(np.float32)


MISC = {}
_at = 0
for _n, _w in (("ident", P), ("causal", P), ("window", P + WIN), ("cmask", T * NB), ("some", T)):
    MISC[_n] = (_at, _at + _w)
    _at += _w
MISCW = _at


class Region:

    def __init__(self, nc, at):
        self.nc, self.at = nc, at

    def __call__(self, name, shape, dt=F32):
        n = 4 if dt != BF16 else 2
        for s in shape[1:]:
            n *= s
        t = self.nc.alloc_sbuf_tensor_at(name, shape, dt, offset=self.at)
        self.at += -(-n // 32) * 32
        return t


def f32(ap):
    return ap.bitcast(F32)


def build(nc, x, wq, wk, wv, wg, wo, wr, br, w1, b1, w2, b2, rope_d, misc_d, late_d, out):
    keep = Region(nc, -(-nc.sbuf_base // 32) * 32)
    misc = keep("misc", [P, MISCW])
    ident_b = keep("ident_b", [P, P], BF16)
    causal_b = keep("causal_b", [P, P], BF16)
    rows_at = keep.at
    gates = keep("gates", [P, H * B, 3, T])
    xt_hi = keep("xt_hi", [P, B, C, N], F32R)
    xt_lo = keep("xt_lo", [P, B, C, N], F32R)
    phase = keep.at
    banks = [nc.alloc_psum_tensor(f"bank{i}", [P, 512], F32) for i in range(8)]
    o_dram = nc.dram_tensor("o_scratch", [H * B, P, N], F32, kind="Internal").ap()

    def m(name):
        a, b = MISC[name]
        return misc[:, a:b]

    normalise(nc, phase, banks, misc, m, ident_b, causal_b, gates, xt_hi, xt_lo, x, wg, misc_d)
    attend(nc, phase, banks, m, ident_b, causal_b, gates, xt_hi, xt_lo, wq, wk, wv, rope_d, o_dram)
    feed_forward(nc, rows_at, banks, m, o_dram, late_d, x, wo, wr, br, w1, b1, w2, b2, out)


def normalise(nc, phase, banks, misc, m, ident_b, causal_b, gates, xt_hi, xt_lo, x, wg, misc_d):
    r = Region(nc, phase)
    gates_v = gates[:].rearrange("p (h b) r t -> p h b r t", b=B)
    xin = r("xin", [P, 2, T, D])
    z = r("z", [P, T, D])
    stats = r("stats", [P, T, 6])
    mv = r("mv", [P, T, 2])
    ve = r("ve", [P, T])
    sd = r("sd", [P, T])
    y = r("y", [P, T])
    yy = r("yy", [P, T])
    ge = r("ge", [P, N])
    gs = r("gs", [P, T, 3 * H])
    wg_raw = r("wg_raw", [P, C, P])
    wg_hi = r("wg_hi", [P, C, P], F32R)
    wg_lo = r("wg_lo", [P, C, P], F32R)
    S = nc.alloc_semaphore
    misc_loaded, wg_zeroed, wg_loaded = S("misc_loaded"), S("wg_zeroed"), S("wg_loaded")
    x_loaded = [S("x_loaded0"), S("x_loaded1")]
    wg_split, masks_ready = S("wg_split"), S("masks_ready")
    stat_step, sd_ready, z_ready, xt_transposed = S("stat_step"), S("sd_ready"), S("z_ready"), S("xt_transposed")
    xt_hi_ready, xt_lo_ready, g_projected, g_exp = S("xt_hi_ready"), S("xt_lo_ready"), S("g_projected"), S("g_exp")
    g_transposed, g_step = S("g_transposed"), S("g_step")
    NSTAT, NG = 4 + 4 + 1 + 5, T + 3

    def steps(eng, body):
        body(0, 0, True, False, False)
        body(1, 1, True, True, False)
        with eng.Fori(1, B // 2) as pair:
            for s in range(2):
                body(pair * 2 + s, s, True, True, True)
        body(B, 0, False, True, True)
        body(B + 1, 1, False, False, True)

    with nc.Block() as block:
        @block.sync
        def _(sp):
            for b in range(B):
                if b >= 2:
                    sp.wait_ge(z_ready, T * (b - 1))
                sp.dma_start(xin[:, b % 2], x[b].rearrange("(t p) d -> p t d", p=P)).then_inc(x_loaded[b % 2], 16)
                if b == 0:
                    sp.dma_start(misc[:], misc_d).then_inc(misc_loaded, 16)
                    sp.wait_ge(wg_zeroed, 1)
                    sp.dma_start(wg_raw[:, :, 0:3 * H], wg.rearrange("(c p) n -> p c n", p=P)).then_inc(wg_loaded, 16)

        @block.gpsimd
        def _(pool):
            nc.gpsimd.memset(wg_raw[:], 0.0).then_inc(wg_zeroed, 1)
            pool.wait_ge(misc_loaded, 16)
            nc.gpsimd.tensor_copy(ident_b[:], m("ident")).then_inc(masks_ready, 1)
            nc.gpsimd.tensor_copy(causal_b[:], m("causal")).then_inc(masks_ready, 1)
            pool.wait_ge(wg_split, 1)
            nc.gpsimd.tensor_tensor(wg_lo[:], wg_raw[:], f32(wg_hi[:]), ALU.subtract).then_inc(wg_split, 1)

        @block.vector
        def _(dve):
            def body(i, s, stat, split, gate):
                if stat:
                    dve.wait_ge(x_loaded[s], (i - s) * 8 + 16)
                    for t in range(T):
                        nc.vector.bn_stats(stats[:, t], xin[:, s, t]).then_inc(stat_step, 1)
                    dve.wait_ge(stat_step, i * NSTAT + 4)
                    nc.vector.memset(yy[:], 0.0)
                    for t in range(T):
                        nc.vector.bn_aggr(mv[:, t], stats[:, t]).then_inc(stat_step, 1)
                    dve.wait_ge(stat_step, i * NSTAT + 8)
                    nc.vector.tensor_scalar(ve[:], mv[:, :, 1], EPS, None, ALU.add).then_inc(stat_step, 1)
                if split:
                    for c in range(C):
                        dve.wait_ge(xt_hi_ready, (i - 1) * C + c + 1)
                        nc.vector.tensor_tensor(xt_lo[:, bass.ds(i - 1, 1), c, :], banks[c][:, :],
                                                f32(xt_hi[:, bass.ds(i - 1, 1), c, :]), ALU.subtract).then_inc(xt_lo_ready, 1)
                if stat:
                    dve.wait_ge(sd_ready, i + 1)
                    nc.vector.reciprocal(y[:], sd[:]).then_inc(stat_step, 1)
                    dve.wait_ge(stat_step, i * NSTAT + 10)
                    nc.vector.tensor_tensor(yy[:], y[:], y[:], ALU.mult).then_inc(stat_step, 1)
                    dve.wait_ge(stat_step, i * NSTAT + 11)
                    nc.vector.tensor_tensor(yy[:], yy[:], ve[:], ALU.mult).then_inc(stat_step, 1)
                    dve.wait_ge(stat_step, i * NSTAT + 12)
                    nc.vector.tensor_scalar(yy[:], yy[:], -0.5, 1.5, ALU.mult, ALU.add).then_inc(stat_step, 1)
                    dve.wait_ge(stat_step, i * NSTAT + 13)
                    nc.vector.tensor_tensor(y[:], yy[:], y[:], ALU.mult).then_inc(stat_step, 1)
                    dve.wait_ge(stat_step, i * NSTAT + 14)
                    for t in range(T):
                        nc.vector.tensor_scalar(z[:, t], xin[:, s, t], mv[:, t, 0:1], y[:, t:t + 1],
                                                ALU.subtract, ALU.mult).then_inc(z_ready, 1)
                if gate:
                    b = i - 2
                    dve.wait_ge(g_transposed, b + 1)
                    nc.vector.tensor_scalar(gs[:], banks[5 + s][:, :].rearrange("p (t n) -> p t n", t=T)[:, :, 0:3 * H],
                                            1.0, None, ALU.add).then_inc(g_step, 1)
                    dve.wait_ge(g_step, b * NG + 1)
                    nc.vector.reciprocal(gs[:], gs[:]).then_inc(g_step, 1)
                    dve.wait_ge(g_step, b * NG + 2)
                    for t in range(T):
                        nc.vector.tensor_scalar(gates_v[:, :, bass.ds(b, 1), :, t].rearrange("p h o r -> p o r h"),
                                                gs[:, t:t + 1].rearrange("p o (r h) -> p o r h", r=3),
                                                1.0, None, ALU.mult).then_inc(g_step, 1)
                    dve.wait_ge(g_step, b * NG + T + 2)
                    gc = gates_v[:, :, bass.ds(b, 1), 0, :].rearrange("p h o t -> p o h t")
                    nc.vector.tensor_tensor(gc, gc, m("some").rearrange("p (o a t) -> p o a t", o=1, a=1).to_broadcast([P, 1, H, T]),
                                            ALU.mult).then_inc(g_step, 1)

            dve.wait_ge(misc_loaded, 16)
            steps(dve, body)

        @block.scalar
        def _(act):
            def body(i, s, stat, split, gate):
                if stat:
                    act.wait_ge(stat_step, i * NSTAT + 9)
                    nc.scalar.activation(sd[:], ve[:], ACT.Sqrt).then_inc(sd_ready, 1)
                if isinstance(i, int) and i == 0:
                    act.wait_ge(wg_loaded, 16)
                    nc.scalar.activation(wg_hi[:], wg_raw[:], ACT.Copy).then_inc(wg_split, 1)
                if stat:
                    for c in range(C):
                        act.wait_ge(xt_transposed, i * C + c + 1)
                        nc.scalar.activation(xt_hi[:, bass.ds(i, 1), c, :], banks[c][:, :], ACT.Copy).then_inc(xt_hi_ready, 1)
                if split:
                    act.wait_ge(g_projected, i)
                    nc.scalar.activation(ge[:, :], banks[4][:, :], ACT.Exp, scale=-1.0).then_inc(g_exp, 1)

            steps(act, body)

        @block.tensor
        def _(pe):
            def body(i, s, stat, split, gate):
                if gate:
                    pe.wait_ge(g_exp, i - 1)
                    if not stat:
                        pe.wait_ge(g_step, (i - 4) * NG + 1)
                    for t in range(T):
                        last = nc.tensor.transpose(banks[5 + s][:, t * P:(t + 1) * P], ge[:, t * P:(t + 1) * P], m("ident"))
                    last.then_inc(g_transposed, 1)
                if stat:
                    pe.wait_ge(z_ready, i * T + T)
                    for c in range(C):
                        for t in range(T):
                            last = nc.tensor.transpose(banks[c][:, t * P:(t + 1) * P], z[:, t, c * P:(c + 1) * P], m("ident"))
                        last.then_inc(xt_transposed, 1)
                if split:
                    pe.wait_ge(xt_lo_ready, i * C)
                    for c in range(C):
                        for w, v in ((wg_hi, xt_hi), (wg_hi, xt_lo), (wg_lo, xt_hi)):
                            last = nc.tensor.matmul(banks[4][:, :], w[:, c, :], v[:, bass.ds(i - 1, 1), c, :],
                                                    start=(c == 0 and w is wg_hi and v is xt_hi), stop=(c == C - 1 and w is wg_lo))
                    last.then_inc(g_projected, 1)

            pe.wait_ge(misc_loaded, 16)
            pe.wait_ge(wg_split, 2)
            steps(pe, body)


def attend(nc, phase, banks, m, ident_b, causal_b, gates, xt_hi, xt_lo, wq, wk, wv, rope_d, o_dram):
    r = Region(nc, phase)
    rope = r("rope", [P, 2, N])
    w_raw = [r(f"w_raw{k}", [P, C, HD]) for k in range(3)]
    w_hi = [r(f"w_hi{k}", [P, C, HD], F32R) for k in range(3)]
    w_lo = [r(f"w_lo{k}", [P, C, HD], F32R) for k in range(3)]
    s_full = [r(f"s_full{k}", [P, N]) for k in range(2)]
    s_swap = [r(f"s_swap{k}", [P, N]) for k in range(2)]
    qk_hi = [r(f"qk_hi{k}", [P, N], F32R) for k in range(2)]
    qk_lo = [r(f"qk_lo{k}", [P, N], F32R) for k in range(2)]
    cosed = [r(f"cosed{k}", [P, N]) for k in range(2)]
    vt = r("vt", [P, N])
    v_hi = r("v_hi", [P, T, HD], F32R)
    v_lo = r("v_lo", [P, T, HD], F32R)
    e1 = r("e1", [P, E1W])
    e2 = r("e2", [P, T, P + WIN])
    pt_hi = r("pt_hi", [P, PTW], F32R)
    pt_lo = r("pt_lo", [P, PTW], F32R)
    o_sb = r("o_sb", [P, N])
    neg1 = r("neg1", [P, T])
    max2 = r("max2", [P, T])
    neg2 = r("neg2", [P, T])
    sc = r("sc", [P, T, NB])
    sc2 = r("sc2", [P, T, NB])
    mc = r("mc", [P, T])
    sums = r("sums", [P, 3, T])
    coef = r("coef", [P, 3, T])
    cb = r("cb", [P, T, NB])
    assert r.at <= nc.sbuf_usable_end, r.at

    S = nc.alloc_semaphore
    rope_loaded = S("rope_loaded")
    w_loaded = [S(f"w{k}_loaded") for k in range(3)]
    w_split = [S(f"w{k}_split") for k in range(3)]
    projected = [S(f"{k}_projected") for k in "qkv"]
    evacuated = [S(f"{k}_evacuated") for k in "qkv"]
    swapped = [S("q_swapped"), S("k_swapped")]
    cos_done = [S("q_cos"), S("k_cos")]
    sin_done = [S("q_sin"), S("k_sin")]
    roped = [S("q_roped"), S("k_roped")]
    hi_done = [S("q_hi_done"), S("k_hi_done")]
    lo_done = [S("q_lo_done"), S("k_lo_done")]
    v_transposed, v_hi_done, v_lo_done = S("v_transposed"), S("v_hi_done"), S("v_lo_done")
    scores_ready, negmax, window_masked, negmax2 = S("scores_ready"), S("negmax"), S("window_masked"), S("negmax2")
    cmp_step, exp_cmp, exp_full, exp_win = S("cmp_step"), S("exp_cmp"), S("exp_full"), S("exp_win")
    win_step = S("win_step")
    mixed, probs_ready = S("mixed"), S("probs_ready")
    pt_ready, pt_hi_done, pt_lo_done = S("pt_ready"), S("pt_hi_done"), S("pt_lo_done")
    out_ready, out_evacuated, out_slot_free, zeros_set = S("out_ready"), S("out_evacuated"), S("out_slot_free"), S("zeros_set")
    NC = T + 3 + 4
    w_dram = [w.rearrange("(c p) n -> p c n", p=P) for w in (wq, wk, wv)]
    QB = [4, 5, 5]

    def steps(eng, body, start=lambda h: None):
        start(0)
        body(0, 0, True, False, False, False)
        body(1, 1, True, True, False, False)
        with eng.Fori(2, B - 1) as b:
            body(b, b, True, True, True, False)
        with eng.Fori(1, H) as h:
            body(h * B - 1, B - 1, True, True, True, h)
            start(h)
            with eng.Fori(0, B - 1) as b:
                body(h * B + b, b, True, True, True, False)
        body(H * B - 1, B - 1, True, True, True, False)
        body(H * B, None, False, True, True, False)
        body(H * B + 1, None, False, False, True, False)

    with nc.Block() as block:
        @block.sync
        def _(sp):
            def load_weights(h):
                for k in range(3):
                    if not isinstance(h, int):
                        sp.wait_ge(w_split[k], h * 2)
                    sp.dma_start(w_raw[k][:], w_dram[k][:, :, bass.ds(h * HD, HD)]).then_inc(w_loaded[k], 16)

            def swap(u, k):
                sp.wait_ge(evacuated[k], u + 1)
                sp.dma_start(s_swap[k][0:64, :], s_full[k][64:128, :]).then_inc(swapped[k], 16)
                sp.dma_start(s_swap[k][64:128, :], s_full[k][0:64, :]).then_inc(swapped[k], 16)

            def body(u, b, project, score, end, split):
                if split is not False:
                    load_weights(split)
                if project:
                    swap(u, 0)
                    swap(u, 1)
                if end:
                    sp.wait_ge(out_evacuated, u)
                    sp.dma_start(o_dram[bass.ds(u - 2, 1)].rearrange("o p n -> p (o n)"), o_sb[:]).then_inc(out_slot_free, 16)

            load_weights(0)
            sp.dma_start(rope[:].rearrange("p a n -> p (a n)"), rope_d).then_inc(rope_loaded, 16)
            steps(sp, body)
            sp.wait_ge(out_slot_free, 16 + 16 * H * B)

        @block.gpsimd
        def _(pool):
            def turn_cos(u, k):
                pool.wait_ge(evacuated[k], u + 1)
                nc.gpsimd.tensor_tensor(cosed[k][:], s_full[k][:], rope[:, 0, :], ALU.mult).then_inc(cos_done[k], 1)

            def turn_sin(u, k):
                pool.wait_ge(swapped[k], u * 32 + 32)
                nc.gpsimd.tensor_tensor(s_swap[k][:], s_swap[k][:], rope[:, 1, :], ALU.mult).then_inc(sin_done[k], 1)
                pool.wait_ge(cos_done[k], u + 1)
                pool.wait_ge(sin_done[k], u + 1)
                nc.gpsimd.tensor_tensor(s_full[k][:], cosed[k][:], s_swap[k][:], ALU.add).then_inc(roped[k], 1)

            def low(u, k):
                pool.wait_ge(hi_done[k], u + 1)
                nc.gpsimd.tensor_tensor(qk_lo[k][:], s_full[k][:], f32(qk_hi[k][:]), ALU.subtract).then_inc(lo_done[k], 1)

            def body(u, b, project, score, end, split):
                if project:
                    for part in (turn_cos, turn_sin, low):
                        for k in range(2):
                            part(u, k)

            nc.gpsimd.memset(o_sb[:], 0.0).then_inc(out_slot_free, 16)
            nc.gpsimd.memset(neg1[:], 0.0).then_inc(out_evacuated, 1)
            pool.wait_ge(rope_loaded, 16)
            steps(pool, body)

        @block.tensor
        def _(pe):
            head = [0]

            def project_one(u, b, k, h2):
                n = 0
                for c in range(C):
                    for w, v in ((w_hi, xt_hi), (w_hi, xt_lo), (w_lo, xt_hi)):
                        last = nc.tensor.matmul(banks[QB[k]][:, :], w[k][:, c, :], v[:, bass.ds(b, 1), c, :],
                                                start=(n == 0), stop=(n == 3 * C - 1))
                        n += 1
                last.then_inc(projected[k], 1)

            def body(u, b, project, score, end, split):
                first = isinstance(u, int) and u < 1
                if project:
                    pe.wait_ge(w_split[0], head[0] * 2 + 2)
                    project_one(u, b, 0, None)
                    pe.wait_ge(w_split[1], head[0] * 2 + 2)
                    if not first:
                        pe.wait_ge(evacuated[2], u)
                    project_one(u, b, 1, None)
                if score:
                    pe.wait_ge(lo_done[0], u)
                    pe.wait_ge(lo_done[1], u)
                    for t in range(T):
                        w = max(256, (t + 1) * P)
                        if end:
                            pe.wait_ge(window_masked, (u - 2) * T + t + 1)
                        for n, (x, v) in enumerate(((qk_hi[0], qk_hi[1]), (qk_hi[0], qk_lo[1]), (qk_lo[0], qk_hi[1]))):
                            nc.tensor.matmul(banks[t][:, 0:w], x[:, t * P:(t + 1) * P], v[:, 0:w], start=(n == 0), stop=(n == 2))
                        nc.tensor.matmul(banks[t][:, t * P:(t + 1) * P], ident_b[:], causal_b[:], start=False, stop=True,
                                         skip_group_check=True).then_inc(scores_ready, 1)
                if end:
                    pe.wait_ge(out_evacuated, u - 1)
                    pe.wait_ge(v_lo_done, u - 1)
                    if project:
                        pe.wait_ge(evacuated[0], u + 1)
                    pe.wait_ge(probs_ready, (u - 2) * T + T)
                    for bank, js in ((6, (0,)), (7, (1,)), (4, (2, 3))):
                        at = 0
                        for j in js:
                            for t in range(j, T):
                                last = nc.tensor.transpose(banks[bank][:, at:at + P],
                                                           e1[:, E1OFF[t] + j * P:E1OFF[t] + (j + 1) * P], m("ident"))
                                at += P
                        last.then_inc(pt_ready, 1)
                if project:
                    pe.wait_ge(w_split[2], head[0] * 2 + 2)
                    pe.wait_ge(evacuated[1], u + 1)
                    project_one(u, b, 2, None)
                if score:
                    pe.wait_ge(evacuated[2], u)
                    if end:
                        pe.wait_ge(pt_lo_done, (u - 2) * 3 + 2)
                    for t in range(T):
                        last = nc.tensor.transpose(banks[7][:, t * P:(t + 1) * P], vt[:, t * P:(t + 1) * P], m("ident"))
                    last.then_inc(v_transposed, 1)
                if end:
                    n = 0
                    for j in range(T):
                        if j < 3:
                            pe.wait_ge(pt_hi_done, (u - 2) * 3 + j + 1)
                            pe.wait_ge(pt_lo_done, (u - 2) * 3 + j + 1)
                        w = N - PTQ0[j]
                        for v, p in ((v_hi, pt_hi), (v_hi, pt_lo), (v_lo, pt_hi)):
                            last = nc.tensor.matmul(banks[6][:, PTQ0[j]:N], v[:, j, :], p[:, PTOFF[j]:PTOFF[j] + w],
                                                    start=(n == 0), stop=(n == 3 * T - 1), skip_group_check=True)
                            n += 1
                    last.then_inc(out_ready, 1)

            def start(h):
                head[0] = h

            pe.wait_ge(zeros_set, 2)
            steps(pe, body, start)

        @block.scalar
        def _(act):
            def evacuate(u, k):
                act.wait_ge(projected[k], u + 1)
                if k < 2 and not (isinstance(u, int) and u == 0):
                    act.wait_ge(lo_done[k], u)
                nc.scalar.activation((s_full[0], s_full[1], vt)[k][:], banks[QB[k]][:, :], ACT.Copy, scale=(HD ** -0.5 if k == 0 else 1.0))\
                    .then_inc(evacuated[k], 1)

            def split_weights(h, k):
                act.wait_ge(w_loaded[k], h * 16 + 16)
                if not isinstance(h, int):
                    act.wait_ge(projected[k], h * B)
                nc.scalar.activation(w_hi[k][:], w_raw[k][:], ACT.Copy).then_inc(w_split[k], 1)

            def high(u, k):
                act.wait_ge(roped[k], u + 1)
                nc.scalar.activation(qk_hi[k][:], s_full[k][:], ACT.Copy).then_inc(hi_done[k], 1)

            def body(u, b, project, score, end, split):
                for k in range(2):
                    if project:
                        evacuate(u, k)
                    if split is not False:
                        split_weights(split, k)
                if end:
                    for g in range(3):
                        w = (512, 384, 384)[g]
                        act.wait_ge(pt_ready, (u - 2) * 3 + g + 1)
                        if g < 2:
                            nc.scalar.activation(pt_hi[:, PTOFF[g]:PTOFF[g] + w], banks[6 + g][:, 0:w], ACT.Copy).then_inc(pt_hi_done, 1)
                        else:
                            nc.scalar.activation(pt_hi[:, PTOFF[2]:PTOFF[2] + 256], banks[4][:, 0:256], ACT.Copy)
                            nc.scalar.activation(pt_hi[:, PTW - P:PTW], banks[4][:, 256:384], ACT.Copy).then_inc(pt_hi_done, 1)
                if score:
                    for t in range(T):
                        w = (t + 1) * P
                        act.wait_ge(negmax, (u - 1) * T + t + 1)
                        nc.scalar.activation(e1[:, E1OFF[t]:E1OFF[t] + w], banks[t][:, 0:w], ACT.Exp, bias=neg1[:, t:t + 1],
                                             accum_out=sums[:, 1, t:t + 1]).then_inc(exp_full, 1)
                if project:
                    high(u, 0)
                    high(u, 1)
                    if score:
                        act.wait_ge(v_transposed, u)
                    evacuate(u, 2)
                if score:
                    act.wait_ge(negmax2, u)
                    for t in range(T):
                        lo = WIN if t == 0 else 0
                        nc.scalar.activation(e2[:, t, lo:], e2[:, t, lo:], ACT.Exp, bias=neg2[:, t:t + 1],
                                             accum_out=sums[:, 2, t:t + 1]).then_inc(exp_win, 1)
                        if t == 1:
                            act.wait_ge(cmp_step, (u - 1) * NC + T + 3)
                            nc.scalar.activation(sc[:], sc2[:], ACT.Exp).then_inc(exp_cmp, 1)
                if end:
                    act.wait_ge(out_ready, u - 1)
                    act.wait_ge(out_slot_free, (u - 2) * 16 + 16)
                    nc.scalar.activation(o_sb[:], banks[6][:, :], ACT.Copy).then_inc(out_evacuated, 1)
                if score:
                    act.wait_ge(v_transposed, u)
                    nc.scalar.activation(v_hi[:].rearrange("p t d -> p (t d)"), banks[7][:, :], ACT.Copy).then_inc(v_hi_done, 1)
                if split is not False:
                    split_weights(split, 2)

            for k in range(3):
                split_weights(0, k)
            steps(act, body)

        @block.vector
        def _(dve):
            def split_weights(h, k):
                dve.wait_ge(w_split[k], h * 2 + 1)
                nc.vector.tensor_tensor(w_lo[k][:], w_raw[k][:], f32(w_hi[k][:]), ALU.subtract).then_inc(w_split[k], 1)

            def mix(t):
                nb = 2 * (t + 1)
                e = e1[:, E1OFF[t]:E1OFF[t] + nb * BS].rearrange("p (n s) -> p n s", s=BS)
                nc.vector.scalar_tensor_tensor(out=e, in0=e, scalar=coef[:, 1, t:t + 1],
                                               in1=cb[:, t, 0:nb].rearrange("p (n o) -> p n o", o=1).to_broadcast([P, nb, BS]),
                                               op0=ALU.mult, op1=ALU.add).then_inc(mixed, 1)

            def mix_window(v, t):
                lo = WIN if t == 0 else 0
                dve.wait_ge(mixed, v * T + t + 1)
                e = e1[:, E1OFF[t] + t * P - WIN + lo:E1OFF[t] + (t + 1) * P]
                nc.vector.scalar_tensor_tensor(out=e, in0=e2[:, t, lo:], scalar=coef[:, 2, t:t + 1], in1=e,
                                               op0=ALU.mult, op1=ALU.add).then_inc(probs_ready, 1)

            def body(u, b, project, score, end, split):
                v = u - 1
                if score:
                    for t in range(T):
                        w = (t + 1) * P
                        dve.wait_ge(scores_ready, v * T + t + 1)
                        nc.vector.reduce_max(neg1[:, t:t + 1], banks[t][:, 0:w], AX.X, negate=True).then_inc(negmax, 1)
                if end:
                    for g in range(3):
                        w = (512, 384, 384)[g]
                        dve.wait_ge(pt_hi_done, (u - 2) * 3 + g + 1)
                        if g < 2:
                            nc.vector.tensor_tensor(pt_lo[:, PTOFF[g]:PTOFF[g] + w], banks[6 + g][:, 0:w],
                                                    f32(pt_hi[:, PTOFF[g]:PTOFF[g] + w]), ALU.subtract).then_inc(pt_lo_done, 1)
                        else:
                            nc.vector.tensor_tensor(pt_lo[:, PTOFF[2]:PTOFF[2] + 256], banks[4][:, 0:256],
                                                    f32(pt_hi[:, PTOFF[2]:PTOFF[2] + 256]), ALU.subtract)
                            nc.vector.tensor_tensor(pt_lo[:, PTW - P:PTW], banks[4][:, 256:384],
                                                    f32(pt_hi[:, PTW - P:PTW]), ALU.subtract).then_inc(pt_lo_done, 1)
                if split is not False:
                    split_weights(split, 0)
                    split_weights(split, 1)
                if score:
                    for t in range(T):
                        nb = 2 * (t + 1)
                        dve.wait_ge(exp_full, v * T + t + 1)
                        nc.vector.reduce_sum(sc[:, t, 0:nb], banks[t][:, 0:nb * BS].rearrange("p (n s) -> p n s", s=BS),
                                             AX.X).then_inc(cmp_step, 1)
                        lo = WIN if t == 0 else 0
                        k0 = t * P - WIN + lo
                        nc.vector.tensor_tensor_reduce(out=e2[:, t, lo:], in0=banks[t][:, k0:(t + 1) * P],
                                                       in1=m("window")[:, lo:], scale=1.0, scalar=-3e38, op0=ALU.add, op1=ALU.max,
                                                       accum_out=max2[:, t:t + 1]).then_inc(window_masked, 1)
                    dve.wait_ge(window_masked, v * T + T)
                    nc.vector.tensor_scalar(neg2[:], max2[:], -1.0, None, ALU.mult).then_inc(negmax2, 1)
                    dve.wait_ge(cmp_step, v * NC + T)
                    nc.vector.scalar_tensor_tensor(out=sc2[:], in0=sc[:], scalar=1.0 / BS,
                                                   in1=m("cmask").rearrange("p (t n) -> p t n", n=NB),
                                                   op0=ALU.mult, op1=ALU.add).then_inc(cmp_step, 1)
                    dve.wait_ge(cmp_step, v * NC + T + 1)
                    nc.vector.reduce_max(mc[:], sc2[:], AX.X).then_inc(cmp_step, 1)
                if score:
                    dve.wait_ge(cmp_step, v * NC + T + 2)
                    nc.vector.tensor_tensor(sc2[:], sc2[:], mc[:].rearrange("p (t o) -> p t o", o=1).to_broadcast([P, T, NB]),
                                            ALU.subtract).then_inc(cmp_step, 1)
                    dve.wait_ge(exp_cmp, v + 1)
                    nc.vector.reduce_sum(sums[:, 0, :], sc[:], AX.X).then_inc(cmp_step, 1)
                    dve.wait_ge(cmp_step, v * NC + T + 4)
                    nc.vector.reciprocal(coef[:, 0:2], sums[:, 0:2]).then_inc(cmp_step, 1)
                    dve.wait_ge(cmp_step, v * NC + T + 5)
                    nc.vector.tensor_tensor(coef[:, 0:2], coef[:, 0:2], gates[:, bass.ds(v, 1), 0:2].rearrange("p o r t -> p (o r) t"),
                                            ALU.mult).then_inc(cmp_step, 1)
                    dve.wait_ge(cmp_step, v * NC + T + 6)
                    nc.vector.tensor_tensor(cb[:], sc[:], coef[:, 0, :].rearrange("p (t o) -> p t o", o=1).to_broadcast([P, T, NB]),
                                            ALU.mult).then_inc(cmp_step, 1)
                    dve.wait_ge(cmp_step, v * NC + T + 7)
                    for t in range(T):
                        mix(t)
                        if t == 0:
                            dve.wait_ge(v_hi_done, v + 1)
                            nc.vector.tensor_tensor(v_lo[:].rearrange("p t d -> p (t d)"), banks[7][:, :],
                                                            f32(v_hi[:].rearrange("p t d -> p (t d)")), ALU.subtract).then_inc(v_lo_done, 1)
                        if t == 1:
                            dve.wait_ge(exp_win, v * T + T)
                            nc.vector.reciprocal(coef[:, 2], sums[:, 2]).then_inc(win_step, 1)
                        if t == 2:
                            dve.wait_ge(win_step, v * 2 + 1)
                            nc.vector.tensor_tensor(coef[:, 2], coef[:, 2], gates[:, bass.ds(v, 1), 2].rearrange("p o t -> p (o t)"),
                                                    ALU.mult).then_inc(win_step, 1)
                    dve.wait_ge(win_step, v * 2 + 2)
                    for t in range(T):
                        mix_window(v, t)
                if split is not False:
                    split_weights(split, 2)

            nc.vector.memset(f32(pt_hi[:, PTOFF[3]:PTOFF[3] + P]), 0.0).then_inc(zeros_set, 1)
            nc.vector.memset(f32(pt_lo[:, PTOFF[3]:PTOFF[3] + P]), 0.0).then_inc(zeros_set, 1)
            nc.vector.memset(sc[:], 0.0).then_inc(zeros_set, 1)
            dve.wait_ge(zeros_set, 3)
            for k in range(3):
                split_weights(0, k)
            steps(dve, body)


def feed_forward(nc, misc_end, banks, m, o_dram, late_d, x, wo, wr, br, w1, b1, w2, b2, out):
    r = Region(nc, misc_end)
    zsel_hi = r("zsel_hi", [P, C, B * P], F32R)
    zsel_lo = r("zsel_lo", [P, C, B * P], F32R)
    place = r("place", [P, B, N], F32R)
    weight = r("weight", [P, B, T])
    base_dram = nc.dram_tensor("base_scratch", [B, P, T, D], F32, kind="Internal").ap()
    project_and_route(nc, r.at, banks, m, o_dram, late_d, x, wo, wr, br, zsel_hi, zsel_lo, place, weight, base_dram)
    experts(nc, r.at, banks, zsel_hi, zsel_lo, place, weight, base_dram, w1, b1, w2, b2, out)


def project_and_route(nc, at, banks, m, o_dram, late_d, x, wo, wr, br, zsel_hi, zsel_lo, place, weight, base_dram):
    r = Region(nc, at)
    G = 4
    K = H // G
    wo_hi, wo_lo = r("wo_hi", [P, H, D], F32R), r("wo_lo", [P, H, D], F32R)
    o_raw = [r(f"o_raw{s}", [P, G, N]) for s in range(2)]
    o_hi = [r(f"o_hi{s}", [P, G, N], F32R) for s in range(2)]
    o_lo = [r(f"o_lo{s}", [P, G, N], F32R) for s in range(2)]
    xin = r("xin2", [P, T, D])
    x1 = r("x1", [P, T, D])
    z2 = r("z2", [P, T, D])
    wr_all = r("wr_all", [P, D])
    late = r("late", [P, 3 * P])
    before, slots, ones = (late[:, k * P:(k + 1) * P] for k in range(3))
    junk = r("junk", [P, D])
    diag = r("diag", [P, N])
    onehot = r("onehot", [P, T, P])
    br_all = r("br_all", [P, 1])
    stats, mv = r("stats2", [P, T, 6]), r("mv2", [P, T, 2])
    ve, sd, y, yy = (r(f"{k}_2", [P, T]) for k in ("ve", "sd", "y", "yy"))
    wraw, wcol, count, sel, unsel, selcum, slot_sb = (r(k, [P, T]) for k in ("wraw", "wcol", "count", "sel", "unsel", "selcum", "slot_sb"))
    assert r.at <= nc.sbuf_usable_end, r.at
    o_v = o_dram.rearrange("(h b) p n -> p h b n", b=B)
    wo_v = wo.rearrange("(k g p) d -> k p g d", p=P, g=G)

    S = nc.alloc_semaphore
    small_loaded = S("small_loaded")
    raw_loaded = [S("raw_loaded0"), S("raw_loaded1")]
    hi_split, lo_split, chunk_used = S("hi_split"), S("lo_split"), S("chunk_used")
    x_loaded, acc_ready, x1_ready = S("x2_loaded"), S("acc_ready"), S("x1_ready")
    step, sd_ready, z2_ready = S("route_step"), S("sd2_ready"), S("z2_ready")
    diag_ready, row_ready, sel_ready, slot_ready = S("diag_ready"), S("row_ready"), S("sel_ready"), S("slot_ready")
    onehot_ready, zsel_ready, place_ready = S("onehot_ready"), S("zsel_ready"), S("place_ready")
    zsel_hi_done, zsel_lo_done, place_done = S("zsel_hi_done"), S("zsel_lo_done"), S("place_done")
    base_ready, base_stored = S("base_ready"), S("base_stored")
    NS = 4 + 4 + 1 + 5 + T + 1 + 1 + T + 1 + 3 + 1

    def batches(eng, body):
        with eng.Fori(0, B - 1) as b:
            body(b, True)
        body(B - 1, False)

    with nc.Block() as block:
        @block.sync
        def _(sp):
            def load_o(b, k):
                sp.wait_ge(lo_split, b * K + K + k - 1)
                sp.dma_start(o_raw[k % 2][:], o_v[:, k * G:(k + 1) * G, bass.ds(b, 1), :].rearrange("p g o n -> p (g o) n"))\
                    .then_inc(raw_loaded[k % 2], 16)

            def load_x(b):
                sp.wait_ge(x1_ready, b * T + 1)
                sp.dma_start(xin[:], x[bass.ds(b, 1)].rearrange("o (t p) d -> p (o t) d", p=P)).then_inc(x_loaded, 16)

            def body(b, more):
                if more:
                    for k in range(K):
                        load_o(b + 1, k)
                        if k == 1:
                            load_x(b + 1)
                sp.wait_ge(base_ready, b * T + T)
                sp.dma_start(base_dram[bass.ds(b, 1)].rearrange("o p t d -> p (o t) d"), x1[:]).then_inc(base_stored, 16)

            for k in range(K):
                if k >= 2:
                    sp.wait_ge(lo_split, k - 1)
                sp.dma_start(o_raw[k % 2][:], wo_v[k]).then_inc(raw_loaded[k % 2], 16)
            sp.dma_start(wr_all[:], wr.rearrange("d o -> o d").to_broadcast([P, D])).then_inc(small_loaded, 16)
            sp.dma_start(late[:], late_d).then_inc(small_loaded, 16)
            sp.dma_start(br_all[:], br.rearrange("(o d) -> o d", o=1).to_broadcast([P, 1])).then_inc(small_loaded, 16)
            for k in range(K):
                load_o(0, k)
            load_x(0)
            batches(sp, body)
            sp.wait_ge(base_stored, 16 + 16 * B)

        @block.scalar
        def _(act):
            def high(b, k):
                act.wait_ge(raw_loaded[k % 2], b * 32 + (k // 2) * 16 + 48)
                act.wait_ge(chunk_used, b * K + k + 1)
                nc.scalar.activation(o_hi[k % 2][:], o_raw[k % 2][:], ACT.Copy).then_inc(hi_split, 1)

            def body(b, more):
                if more:
                    high(b + 1, 0)
                    high(b + 1, 1)
                act.wait_ge(step, b * NS + 9)
                nc.scalar.activation(sd[:], ve[:], ACT.Sqrt).then_inc(sd_ready, 1)
                if more:
                    high(b + 1, 2)
                    high(b + 1, 3)
                act.wait_ge(zsel_ready, b + 1)
                nc.scalar.activation(zsel_hi[:, :, bass.ds(b * P, P)], banks[6][:, :].rearrange("p (c s) -> p c s", c=C),
                                     ACT.Copy).then_inc(zsel_hi_done, 1)
                act.wait_ge(place_ready, b + 1)
                nc.scalar.activation(place[:, bass.ds(b, 1), :], banks[7][:, :], ACT.Copy).then_inc(place_done, 1)

            for k in range(K):
                act.wait_ge(raw_loaded[k % 2], k // 2 * 16 + 16)
                nc.scalar.activation(wo_hi[:, k * G:(k + 1) * G, :], o_raw[k % 2][:], ACT.Copy).then_inc(hi_split, 1)
            for k in range(K):
                high(0, k)
            batches(act, body)

        @block.gpsimd
        def _(pool):
            def low(b, k):
                pool.wait_ge(hi_split, b * K + K + k + 1)
                nc.gpsimd.tensor_tensor(o_lo[k % 2][:], o_raw[k % 2][:], f32(o_hi[k % 2][:]), ALU.subtract).then_inc(lo_split, 1)

            nc.gpsimd.memset(y[:], 0.0).then_inc(chunk_used, 1)
            nc.gpsimd.memset(yy[:], 0.0).then_inc(chunk_used, 1)
            nc.gpsimd.memset(sd[:], 0.0).then_inc(x1_ready, 1)
            nc.gpsimd.memset(ve[:], 0.0).then_inc(base_stored, 16)
            for k in range(K):
                pool.wait_ge(hi_split, k + 1)
                nc.gpsimd.tensor_tensor(wo_lo[:, k * G:(k + 1) * G, :], o_raw[k % 2][:], f32(wo_hi[:, k * G:(k + 1) * G, :]),
                                        ALU.subtract).then_inc(lo_split, 1)
            for k in range(K):
                low(0, k)
            with pool.Fori(0, B - 1) as b:
                for k in range(K):
                    low(b + 1, k)

        @block.tensor
        def _(pe):
            def chunk(b, k, first=False):
                pe.wait_ge(lo_split, b * K + K + k + 1)
                for t in range(T):
                    if k == 0 and not first:
                        pe.wait_ge(x1_ready, b * T + (t - 2))
                    n = 0
                    for g in range(G):
                        for o, w in ((o_hi, wo_hi), (o_hi, wo_lo), (o_lo, wo_hi)):
                            last = nc.tensor.matmul(banks[t][:, :], o[k % 2][:, g, t * P:(t + 1) * P], w[:, k * G + g, :],
                                                    start=(k == 0 and n == 0), stop=(k == K - 1 and n == 3 * G - 1))
                            n += 1
                    if k == K - 1 and t < T - 1:
                        last.then_inc(acc_ready, 1)
                last.then_inc(chunk_used, 1)

            def body(b, more):
                if more:
                    chunk(b + 1, 0)
                pe.wait_ge(diag_ready, b * T + T)
                nc.tensor.matmul(banks[4][:, :], ones, diag[:], start=True, stop=True).then_inc(row_ready, 1)
                if more:
                    chunk(b + 1, 1)
                pe.wait_ge(sel_ready, b + 1)
                nc.tensor.matmul(banks[5][:, 0:T], before, sel[:], start=True, stop=False)
                nc.tensor.matmul(banks[5][:, 0:T], ones, selcum[:], start=False, stop=True).then_inc(slot_ready, 1)
                if more:
                    chunk(b + 1, 2)
                pe.wait_ge(onehot_ready, b * T + T)
                for c in range(C):
                    for t in range(T):
                        last = nc.tensor.matmul(banks[6][:, c * P:(c + 1) * P], z2[:, t, c * P:(c + 1) * P], onehot[:, t, :],
                                                start=(t == 0), stop=(t == T - 1))
                last.then_inc(zsel_ready, 1)
                for t in range(T):
                    last = nc.tensor.transpose(banks[7][:, t * P:(t + 1) * P], onehot[:, t, :], m("ident"))
                last.then_inc(place_ready, 1)
                if more:
                    chunk(b + 1, 3)

            for k in range(K):
                chunk(0, k, first=True)
            batches(pe, body)

        @block.vector
        def _(dve):
            v = nc.vector

            def body(b, more):
                at = [0]

                def after():
                    dve.wait_ge(step, b * NS + at[0])

                def did(ins):
                    ins.then_inc(step, 1)
                    at[0] += 1

                dve.wait_ge(x_loaded, b * 16 + 16)
                dve.wait_ge(base_stored, b * 16 + 16)
                for t in range(T):
                    if t < T - 1:
                        dve.wait_ge(acc_ready, b * (T - 1) + t + 1)
                    else:
                        dve.wait_ge(chunk_used, b * K + K + 2)
                    v.tensor_tensor(x1[:, t], xin[:, t], banks[t][:, :], ALU.add).then_inc(x1_ready, 1)
                for t in range(T):
                    dve.wait_ge(x1_ready, b * T + t + 2)
                    did(v.bn_stats(stats[:, t], x1[:, t]))
                after()
                v.memset(yy[:], 0.0)
                for t in range(T):
                    did(v.bn_aggr(mv[:, t], stats[:, t]))
                after()
                did(v.tensor_scalar(ve[:], mv[:, :, 1], EPS, None, ALU.add))
                dve.wait_ge(sd_ready, b + 1)
                did(v.reciprocal(y[:], sd[:]))
                after()
                did(v.tensor_tensor(yy[:], y[:], y[:], ALU.mult))
                after()
                did(v.tensor_tensor(yy[:], yy[:], ve[:], ALU.mult))
                after()
                did(v.tensor_scalar(yy[:], yy[:], -0.5, 1.5, ALU.mult, ALU.add))
                after()
                did(v.tensor_tensor(y[:], yy[:], y[:], ALU.mult))
                after()
                for t in range(T):
                    v.tensor_scalar(z2[:, t], x1[:, t], mv[:, t, 0:1], y[:, t:t + 1], ALU.subtract, ALU.mult).then_inc(z2_ready, 1)
                dve.wait_ge(small_loaded, 48)
                for t in range(T):
                    dve.wait_ge(z2_ready, b * T + t + 1)
                    after()
                    did(v.tensor_tensor_reduce(out=junk[:], in0=z2[:, t], in1=wr_all[:], scale=1.0, scalar=0.0,
                                               op0=ALU.mult, op1=ALU.add, accum_out=wraw[:, t:t + 1]))
                after()
                did(v.tensor_scalar(wcol[:], wraw[:], br_all[:, 0:1], None, ALU.add))
                did(v.tensor_scalar(weight[:, bass.ds(b, 1), :], wraw[:].rearrange("p (o t) -> p o t", o=1), br_all[:, 0:1], None, ALU.add))
                after()
                for t in range(T):
                    v.tensor_scalar(diag[:, t * P:(t + 1) * P], m("ident"), wcol[:, t:t + 1], None, ALU.mult).then_inc(diag_ready, 1)
                dve.wait_ge(row_ready, b + 1)
                for t in range(T):
                    after()
                    did(v.tensor_scalar(junk[:], banks[4][:, :], wcol[:, t:t + 1], None, ALU.is_ge, ALU.add,
                                        accum_out=count[:, t:t + 1]))
                after()
                did(v.tensor_scalar(sel[:], count[:], float(KTOP), None, ALU.is_lt))
                after()
                did(v.tensor_copy(selcum[:, 1:2], sel[:, 0:1]))
                v.tensor_scalar(unsel[:], sel[:], -1.0, 1.0, ALU.mult, ALU.add).then_inc(step, 1)
                at[0] += 1
                after()
                did(v.tensor_tensor(selcum[:, 2:3], selcum[:, 1:2], sel[:, 1:2], ALU.add))
                after()
                v.tensor_tensor(selcum[:, 3:4], selcum[:, 2:3], sel[:, 2:3], ALU.add).then_inc(sel_ready, 1)
                for t in range(T):
                    v.scalar_tensor_tensor(out=x1[:, t], in0=z2[:, t], scalar=unsel[:, t:t + 1], in1=x1[:, t],
                                           op0=ALU.mult, op1=ALU.add).then_inc(base_ready, 1)
                dve.wait_ge(slot_ready, b + 1)
                did(v.tensor_copy(slot_sb[:], banks[5][:, 0:T]))
                after()
                for t in range(T):
                    v.tensor_scalar(onehot[:, t], slots, slot_sb[:, t:t + 1], sel[:, t:t + 1],
                                    ALU.is_equal, ALU.mult).then_inc(onehot_ready, 1)
                dve.wait_ge(zsel_hi_done, b + 1)
                v.tensor_tensor(zsel_lo[:, :, bass.ds(b * P, P)], banks[6][:, :].rearrange("p (c s) -> p c s", c=C),
                                f32(zsel_hi[:, :, bass.ds(b * P, P)]), ALU.subtract).then_inc(zsel_lo_done, 1)
                assert at[0] == NS, (at[0], NS)

            v.memset(selcum[:], 0.0)
            batches(dve, body)


def experts(nc, at, banks, zsel_hi, zsel_lo, place, weight, base_dram, w1, b1, w2, b2, out):
    r = Region(nc, at)
    GB = 4
    NG = B // GB
    w1_raw, w2_raw = ([r(f"{n}{s}", [P, 512]) for s in range(2)] for n in ("w1_raw", "w2_raw"))
    w1_hi, w1_lo, w2_hi, w2_lo = ([r(f"{n}{s}", [P, 512], F32R) for s in range(2)] for n in ("w1_hi", "w1_lo", "w2_hi", "w2_lo"))
    b1_sb = r("b1_sb", [P, FT])
    b2_all = r("b2_all", [P, D])
    hid = [r(f"hid{s}", [P, GB * P]) for s in range(2)]
    hid_hi = [r(f"hid_hi{s}", [P, GB * P], F32R) for s in range(2)]
    hid_lo = [r(f"hid_lo{s}", [P, GB * P], F32R) for s in range(2)]
    ff = r("ff", [P, GB, D])
    ff_hi, ff_lo = r("ff_hi", [P, GB, D], F32R), r("ff_lo", [P, GB, D], F32R)
    base = [r(f"base{s}", [P, T, D]) for s in range(2)]
    assert r.at <= nc.sbuf_usable_end, r.at
    w1_v = w1.rearrange("(c p) f -> p c f", p=P)
    w2_v = w2.rearrange("(f p) d -> f p d", p=P)

    S = nc.alloc_semaphore
    bias_loaded = S("bias_loaded")
    w_loaded = [S("w12_loaded0"), S("w12_loaded1")]
    w1_hi_done, w1_lo_done, w2_hi_done, w2_lo_done = S("w1_hi_done"), S("w1_lo_done"), S("w2_hi_done"), S("w2_lo_done")
    hid_ready, gelu_done, hid_hi_done, hid_lo_done = S("hid_ready"), S("gelu_done"), S("hid_hi_done"), S("hid_lo_done")
    step_done, ffacc_ready, ff_ready = S("step_done"), S("ffacc_ready"), S("ff_ready")
    ff_hi_done, ff_lo_done = S("ff_hi_done"), S("ff_lo_done")
    spread_ready, final_ready, stored = S("spread_ready"), S("final_ready"), S("stored")
    base_loaded = [S("base_loaded0"), S("base_loaded1")]

    def tiles(eng, g, body):
        at = g * FT // 2
        for s in range(2):
            body(at, s, s, s == 0, False)
        with eng.Fori(1, FT // 2 - 1) as pair:
            for s in range(2):
                body(pair + at, s, pair * 2 + s, False, False)
        for s in range(2):
            body(at + FT // 2 - 1, s, FT - 2 + s, False, s == 1)

    with nc.Block() as block:
        @block.sync
        def _(sp):
            def load(pair, s, f, first, last):
                if isinstance(pair, int) and pair and pair % (FT // 2) == 0 and not last:
                    return
                load_ahead(pair, s, f)

            def load_ahead(pair, s, f):
                if not (isinstance(pair, int) and pair == 0):
                    sp.wait_ge(w1_lo_done, pair * 2 + s - 1)
                    sp.wait_ge(w2_lo_done, pair * 2 + s - 1)
                sp.dma_start(w1_raw[s][:].rearrange("p (c f) -> p c f", c=C), w1_v[:, :, bass.ds(f * P, P)]).then_inc(w_loaded[s], 16)
                sp.dma_start(w2_raw[s][:], w2_v[bass.ds(f, 1)].rearrange("o p d -> p (o d)")).then_inc(w_loaded[s], 16)

            def load_base(b):
                if b >= 2:
                    sp.wait_ge(stored, 16 * (b - 1))
                sp.dma_start(base[b % 2][:], base_dram[b]).then_inc(base_loaded[b % 2], 16)

            sp.dma_start(b1_sb[:], b1).then_inc(bias_loaded, 16)
            sp.dma_start(b2_all[:], b2.rearrange("(o d) -> o d", o=1).to_broadcast([P, D])).then_inc(bias_loaded, 16)
            load_base(0)
            load_base(1)
            for g in range(NG):
                tiles(sp, g, load)
                if g + 1 < NG:
                    for s in range(2):
                        load_ahead((g + 1) * FT // 2, s, s)
                for b in range(g * GB, (g + 1) * GB):
                    sp.wait_ge(final_ready, (b + 1) * T)
                    sp.dma_start(out[b].rearrange("(t p) d -> p t d", p=P), base[b % 2][:]).then_inc(stored, 16)
                    if b + 2 < B:
                        load_base(b + 2)
            sp.wait_ge(stored, 16 * B)

        @block.gpsimd
        def _(pool):
            def low(pair, s, f, first, last):
                for raw, hi, lo, hi_done, lo_done in ((w1_raw, w1_hi, w1_lo, w1_hi_done, w1_lo_done),
                                                      (w2_raw, w2_hi, w2_lo, w2_hi_done, w2_lo_done)):
                    pool.wait_ge(hi_done, pair * 2 + s + 1)
                    nc.gpsimd.tensor_tensor(lo[s][:], raw[s][:], f32(hi[s][:]), ALU.subtract).then_inc(lo_done, 1)

            for g in range(NG):
                tiles(pool, g, low)

        @block.scalar
        def _(act):
            def high(which, pair, s):
                raw, hi, done = ((w1_raw, w1_hi, w1_hi_done), (w2_raw, w2_hi, w2_hi_done))[which]
                act.wait_ge(w_loaded[s], pair * 32 + 32)
                if not (isinstance(pair, int) and pair == 0):
                    act.wait_ge((hid_ready, step_done)[which], pair * 2 + s - 1)
                nc.scalar.activation(hi[s][:], raw[s][:], ACT.Copy).then_inc(done, 1)

            def body(pair, s, f, first, last):
                nxt = (pair + s, 1 - s)
                end = last and pair == B * P * FT // (GB * P) // 2 - 1
                if not end:
                    high(0, *nxt)
                act.wait_ge(hid_ready, pair * 2 + s + 1)
                nc.scalar.activation(hid[s][:], banks[4 + s][:, :], ACT.Gelu_apprx_tanh, bias=b1_sb[:, bass.ds(f, 1)]).then_inc(gelu_done, 1)
                act.wait_ge(gelu_done, pair * 2 + s + 1)
                nc.scalar.activation(hid_hi[s][:], hid[s][:], ACT.Copy).then_inc(hid_hi_done, 1)
                if not end:
                    high(1, *nxt)

            act.wait_ge(bias_loaded, 32)
            high(0, 0, 0)
            high(1, 0, 0)
            for g in range(NG):
                tiles(act, g, body)
                for q in range(GB):
                    act.wait_ge(ff_ready, g * GB + q + 1)
                    nc.scalar.activation(ff_hi[:, q], ff[:, q], ACT.Copy).then_inc(ff_hi_done, 1)

        @block.tensor
        def _(pe):
            def hidden(g, pair, s):
                pe.wait_ge(w1_lo_done, pair * 2 + s + 1)
                k = 0
                for c in range(C):
                    for w, z in ((w1_hi, zsel_hi), (w1_hi, zsel_lo), (w1_lo, zsel_hi)):
                        last = nc.tensor.matmul(banks[4 + s][:, :], w[s][:, c * P:(c + 1) * P], z[:, c, g * GB * P:(g + 1) * GB * P],
                                                start=(k == 0), stop=(k == 3 * C - 1))
                        k += 1
                last.then_inc(hid_ready, 1)

            for g in range(NG):
                def body(pair, s, f, first, last):
                    if not last:
                        hidden(g, pair + s, 1 - s)
                    pe.wait_ge(w2_lo_done, pair * 2 + s + 1)
                    pe.wait_ge(hid_lo_done, pair * 2 + s + 1)
                    for q in range(GB):
                        for k, (h, w) in enumerate(((hid_hi, w2_hi), (hid_hi, w2_lo), (hid_lo, w2_hi))):
                            ins = nc.tensor.matmul(banks[q][:, :], h[s][:, q * P:(q + 1) * P], w[s][:],
                                                   start=(first and k == 0), stop=(last and k == 2))
                        if last and q < GB - 1:
                            ins.then_inc(ffacc_ready, 1)
                    ins.then_inc(step_done, 1)

                if g:
                    pe.wait_ge(ff_ready, g * GB)
                    pe.wait_ge(final_ready, g * GB * T)
                hidden(g, g * FT // 2, 0)
                tiles(pe, g, body)
                for q in range(GB):
                    b = g * GB + q
                    pe.wait_ge(ff_lo_done, b + 1)
                    for t in range(T):
                        if q:
                            pe.wait_ge(final_ready, (b - 1) * T + t + 1)
                        for k, v in enumerate((ff_hi, ff_lo)):
                            last = nc.tensor.matmul(banks[4 + t][:, :], place[:, b, t * P:(t + 1) * P], v[:, q],
                                                    start=(k == 0), stop=(k == 1))
                        last.then_inc(spread_ready, 1)

        @block.vector
        def _(dve):
            def low(pair, s, f, first, last):
                dve.wait_ge(hid_hi_done, pair * 2 + s + 1)
                nc.vector.tensor_tensor(hid_lo[s][:], hid[s][:], f32(hid_hi[s][:]), ALU.subtract).then_inc(hid_lo_done, 1)

            dve.wait_ge(bias_loaded, 32)
            for g in range(NG):
                tiles(dve, g, low)
                for q in range(GB):
                    if q < GB - 1:
                        dve.wait_ge(ffacc_ready, g * (GB - 1) + q + 1)
                    else:
                        dve.wait_ge(step_done, (g + 1) * FT)
                    nc.vector.tensor_tensor(ff[:, q], banks[q][:, :], b2_all[:], ALU.add).then_inc(ff_ready, 1)
                for q in range(GB):
                    dve.wait_ge(ff_hi_done, g * GB + q + 1)
                    nc.vector.tensor_tensor(ff_lo[:, q], ff[:, q], f32(ff_hi[:, q]), ALU.subtract).then_inc(ff_lo_done, 1)
                for q in range(GB):
                    b = g * GB + q
                    dve.wait_ge(base_loaded[b % 2], 16 * (b // 2 + 1))
                    for t in range(T):
                        dve.wait_ge(spread_ready, b * T + t + 1)
                        nc.vector.scalar_tensor_tensor(out=base[b % 2][:, t], in0=banks[4 + t][:, :], scalar=weight[:, b, t:t + 1],
                                                       in1=base[b % 2][:, t], op0=ALU.mult, op1=ALU.add).then_inc(final_ready, 1)


_INS = ["L0_attn_x", "L0_attn_Wq", "L0_attn_Wk", "L0_attn_Wv", "L0_attn_Wg", "L0_attn_Wo", "L0_ffn_W_r", "L0_ffn_b_r",
        "L0_ffn_W1", "L0_ffn_b1", "L0_ffn_W2", "L0_ffn_b2"]


def given(inputs):
    a = {n: np.ascontiguousarray(inputs[n]) for n in _INS}
    a["L0_ffn_b1"] = np.ascontiguousarray(a["L0_ffn_b1"].reshape(FT, P).T)
    a["rope"], a["misc"], a["late"] = consts()
    return a


def kernel(**inputs):
    import concourse.bacc as bacc
    from concourse.bass_utils import run_bass_kernel_spmd

    nc = bacc.Bacc("TRN2", target_bir_lowering=False, num_devices=1)
    arrays, args = {}, []
    for name, a in given(inputs).items():
        arrays[f"in_{name}"] = a
        args.append(nc.dram_tensor(f"in_{name}", a.shape, mybir.dt.from_np(a.dtype), kind="ExternalInput").ap())
    out = nc.dram_tensor("out", (B, N, D), F32, kind="ExternalOutput").ap()
    build(nc, *args, out)
    r = run_bass_kernel_spmd(nc, [arrays], core_ids=[0])
    return r.results[0]["out"]
```

```python
import numpy as np
import concourse.bass as bass
from concourse import mybir
from concourse.alu_op_type import AluOpType as ALU

B, N, D = 8, 512, 512
H, HD = 16, 128
BS = 64
NB = N // BS
WIN = 64
DFF = 4 * 512
KTOP = int(0.125 * 1024)
EPS = 1e-5
NEG = -1e30
P = 128
T = N // P
C = D // P
FT = DFF // P
EARLY = 4
BASE = 10000.0

F32, F32R = mybir.dt.float32, mybir.dt.float32r
ACT = mybir.ActivationFunctionType
AX = mybir.AxisListType

E1OFF = [0, 128, 384, 768]
E1W = 1280
PTOFF = [0, 512, 896, 1152]
PTQ0 = [0, 128, 256, 256]
PTW = 1408


def consts():
    half = HD // 2
    inv = (np.float32(1.0) / np.float32(BASE) ** (np.arange(half, dtype=np.float32) / np.float32(half))).astype(np.float32)
    th = (np.arange(N, dtype=np.float32)[:, None] * inv[None, :]).astype(np.float32)
    cos, sin = np.cos(th).T.astype(np.float32), np.sin(th).T.astype(np.float32)
    cosk = np.concatenate([cos, cos])
    sink = np.concatenate([-sin, sin])
    rope = np.stack([cosk, sink], 1)
    p = np.arange(P)
    ident = np.eye(P)
    causal = np.where(p[None, :] <= p[:, None], 0.0, NEG)
    c = np.arange(P + WIN)
    window = np.where((c[None, :] <= p[:, None] + WIN) & (c[None, :] >= p[:, None]), 0.0, NEG)
    q = p[:, None] + P * np.arange(T)[None, :]
    ends = (np.arange(NB) + 1) * BS - 1
    cmask = np.where(q[:, :, None] >= ends, 0.0, NEG)
    some = (q >= ends[0]) / BS
    before = np.where(p[:, None] < p[None, :], 1.0, 0.0)
    slot = np.broadcast_to(p[None, :], (P, P))
    ones = np.ones((P, P))
    misc = np.concatenate([x.reshape(P, -1) for x in (ident, causal, window, cmask, some)], 1)
    late = np.concatenate([before, slot, ones], 1)
    return rope.reshape(P, -1).astype(np.float32), misc.astype(np.float32), late.astype(np.float32)


MISC = {}
_at = 0
for _n, _w in (("ident", P), ("causal", P), ("window", P + WIN), ("cmask", T * NB), ("some", T)):
    MISC[_n] = (_at, _at + _w)
    _at += _w
MISCW = _at


class Region:

    def __init__(self, nc, at):
        self.nc, self.at = nc, at

    def __call__(self, name, shape, dt=F32):
        n = 4
        for s in shape[1:]:
            n *= s
        t = self.nc.alloc_sbuf_tensor_at(name, shape, dt, offset=self.at)
        self.at += -(-n // 32) * 32
        return t


def f32(ap):
    return ap.bitcast(F32)


def build(nc, x, wq, wk, wv, wg, wo, wr, br, w1, b1, w2, b2, rope_d, misc_d, late_d, out):
    keep = Region(nc, -(-nc.sbuf_base // 32) * 32)
    misc = keep("misc", [P, MISCW])
    gates = keep("gates", [P, H * B, 3, T])
    xt_at = keep.at
    xt_hi = keep("xt_hi", [P, B, C, N], F32R)
    xt_lo = keep("xt_lo", [P, B, C, N], F32R)
    phase = keep.at
    banks = [nc.alloc_psum_tensor(f"bank{i}", [P, 512], F32) for i in range(8)]
    o_dram = nc.dram_tensor("o_scratch", [H * B, P, N], F32, kind="Internal").ap()

    def m(name):
        a, b = MISC[name]
        return misc[:, a:b]

    qkv = Region(nc, phase)
    weights = Weights(nc, qkv, wq, wk, wv)
    phase = qkv.at
    normalise(nc, phase, banks, misc, m, gates, xt_hi, xt_lo, x, wg, misc_d, weights)
    chunks = Chunks(nc, Region(nc, xt_at), wo, o_dram)
    attend(nc, phase, banks, m, gates, xt_hi, xt_lo, weights, rope_d, o_dram, chunks)
    project_and_route(nc, xt_at, chunks, banks, m, late_d, x, wr, br, w1, b1, w2, b2, out)


class Weights:

    def __init__(self, nc, r, wq, wk, wv):
        self.nc = nc
        self.raw = [r(f"w_raw{k}", [P, C, HD]) for k in range(3)]
        self.hi = [r(f"w_hi{k}", [P, C, HD], F32R) for k in range(3)]
        self.lo = [r(f"w_lo{k}", [P, C, HD], F32R) for k in range(3)]
        self.dram = [w.rearrange("(c p) n -> p c n", p=P) for w in (wq, wk, wv)]
        self.loaded = [nc.alloc_semaphore(f"w{k}_loaded") for k in range(3)]
        self.split = [nc.alloc_semaphore(f"w{k}_split") for k in range(3)]

    def load(self, sp, h):
        for k in range(3):
            if not isinstance(h, int):
                sp.wait_ge(self.split[k], h * 2)
            sp.dma_start(self.raw[k][:], self.dram[k][:, :, bass.ds(h * HD, HD)]).then_inc(self.loaded[k], 16)

    def high(self, act, h, k):
        act.wait_ge(self.loaded[k], h * 16 + 16)
        self.nc.scalar.activation(self.hi[k][:], self.raw[k][:], ACT.Copy).then_inc(self.split[k], 1)

    def low(self, dve, h, k):
        dve.wait_ge(self.split[k], h * 2 + 1)
        self.nc.vector.tensor_tensor(self.lo[k][:], self.raw[k][:], f32(self.hi[k][:]), ALU.subtract).then_inc(self.split[k], 1)


def normalise(nc, phase, banks, misc, m, gates, xt_hi, xt_lo, x, wg, misc_d, weights):
    r = Region(nc, phase)
    gates_v = gates[:].rearrange("p (h b) r t -> p h b r t", b=B)
    xin = r("xin", [P, 2, T, D])
    z = r("z", [P, T, D])
    stats = r("stats", [P, T, 6])
    mv = r("mv", [P, T, 2])
    ve = r("ve", [P, T])
    sd = r("sd", [P, T])
    y = r("y", [P, T])
    minus = r("minus", [P, T])
    yy = r("yy", [P, T])
    ge = r("ge", [P, N])
    wg_raw = r("wg_raw", [P, C, P])
    wg_hi = r("wg_hi", [P, C, P], F32R)
    wg_lo = r("wg_lo", [P, C, P], F32R)
    S = nc.alloc_semaphore
    misc_loaded, wg_zeroed, wg_loaded = S("misc_loaded"), S("wg_zeroed"), S("wg_loaded")
    x_loaded = [S("x_loaded0"), S("x_loaded1")]
    wg_split = S("wg_split")
    stat_step, sd_ready, z_ready, xt_transposed = S("stat_step"), S("sd_ready"), S("z_ready"), S("xt_transposed")
    xt_hi_ready, xt_lo_ready, g_projected, g_squashed = S("xt_hi_ready"), S("xt_lo_ready"), S("g_projected"), S("g_squashed")
    g_transposed, g_step = S("g_transposed"), S("g_step")
    NSTAT, NG = 4 + 4 + 1 + 6, T + 1

    def steps(eng, body):
        body(0, 0, True, False, False)
        body(1, 1, True, True, False)
        with eng.Fori(1, B // 2) as pair:
            for s in range(2):
                body(pair * 2 + s, s, True, True, True)
        body(B, 0, False, True, True)
        body(B + 1, 1, False, False, True)

    with nc.Block() as block:
        @block.sync
        def _(sp):
            for b in range(B):
                if b >= 2:
                    sp.wait_ge(z_ready, T * (b - 1))
                sp.dma_start(xin[:, b % 2], x[b].rearrange("(t p) d -> p t d", p=P)).then_inc(x_loaded[b % 2], 16)
                if b == 0:
                    sp.dma_start(misc[:], misc_d).then_inc(misc_loaded, 16)
                    sp.wait_ge(wg_zeroed, 1)
                    sp.dma_start(wg_raw[:, :, 0:3 * H], wg.rearrange("(c p) n -> p c n", p=P)).then_inc(wg_loaded, 16)
            weights.load(sp, 0)

        @block.gpsimd
        def _(pool):
            nc.gpsimd.memset(wg_raw[:], 0.0).then_inc(wg_zeroed, 1)
            pool.wait_ge(wg_split, 1)
            nc.gpsimd.tensor_tensor(wg_lo[:], wg_raw[:], f32(wg_hi[:]), ALU.subtract).then_inc(wg_split, 1)

        @block.vector
        def _(dve):
            def body(i, s, stat, split, gate):
                if stat:
                    dve.wait_ge(x_loaded[s], (i - s) * 8 + 16)
                    for t in range(T):
                        nc.vector.bn_stats(stats[:, t], xin[:, s, t]).then_inc(stat_step, 1)
                    dve.wait_ge(stat_step, i * NSTAT + 4)
                    nc.vector.memset(yy[:], 0.0)
                    for t in range(T):
                        nc.vector.bn_aggr(mv[:, t], stats[:, t]).then_inc(stat_step, 1)
                    dve.wait_ge(stat_step, i * NSTAT + 8)
                    nc.vector.tensor_scalar(ve[:], mv[:, :, 1], EPS, None, ALU.add).then_inc(stat_step, 1)
                if split:
                    for c in range(C):
                        dve.wait_ge(xt_hi_ready, (i - 1) * C + c + 1)
                        nc.vector.tensor_tensor(xt_lo[:, bass.ds(i - 1, 1), c, :], banks[c][:, :],
                                                f32(xt_hi[:, bass.ds(i - 1, 1), c, :]), ALU.subtract).then_inc(xt_lo_ready, 1)
                if stat:
                    dve.wait_ge(sd_ready, i + 1)
                    nc.vector.reciprocal(y[:], sd[:]).then_inc(stat_step, 1)
                    dve.wait_ge(stat_step, i * NSTAT + 10)
                    nc.vector.tensor_tensor(yy[:], y[:], y[:], ALU.mult).then_inc(stat_step, 1)
                    dve.wait_ge(stat_step, i * NSTAT + 11)
                    nc.vector.tensor_tensor(yy[:], yy[:], ve[:], ALU.mult).then_inc(stat_step, 1)
                    dve.wait_ge(stat_step, i * NSTAT + 12)
                    nc.vector.tensor_scalar(yy[:], yy[:], -0.5, 1.5, ALU.mult, ALU.add).then_inc(stat_step, 1)
                    dve.wait_ge(stat_step, i * NSTAT + 13)
                    nc.vector.tensor_tensor(y[:], yy[:], y[:], ALU.mult).then_inc(stat_step, 1)
                    dve.wait_ge(stat_step, i * NSTAT + 14)
                    nc.vector.scalar_tensor_tensor(out=minus[:], in0=mv[:, :, 0], scalar=-1.0, in1=y[:],
                                                   op0=ALU.mult, op1=ALU.mult).then_inc(stat_step, 1)
                if gate:
                    b = i - 2
                    dve.wait_ge(g_transposed, b + 1)
                    for t in range(T):
                        nc.vector.tensor_scalar(gates_v[:, :, bass.ds(b, 1), :, t].rearrange("p h o r -> p o r h"),
                                                banks[5 + s][:, t * P:t * P + 3 * H].rearrange("p (o r h) -> p o r h", o=1, r=3),
                                                1.0, None, ALU.mult).then_inc(g_step, 1)
                    dve.wait_ge(g_step, b * NG + T)
                    gc = gates_v[:, :, bass.ds(b, 1), 0, :].rearrange("p h o t -> p o h t")
                    nc.vector.tensor_tensor(gc, gc, m("some").rearrange("p (o a t) -> p o a t", o=1, a=1).to_broadcast([P, 1, H, T]),
                                            ALU.mult).then_inc(g_step, 1)

            dve.wait_ge(misc_loaded, 16)
            steps(dve, body)
            for k in range(3):
                weights.low(dve, 0, k)

        @block.scalar
        def _(act):
            def body(i, s, stat, split, gate):
                if stat:
                    act.wait_ge(stat_step, i * NSTAT + 9)
                    nc.scalar.activation(sd[:], ve[:], ACT.Sqrt).then_inc(sd_ready, 1)
                if isinstance(i, int) and i == 0:
                    act.wait_ge(wg_loaded, 16)
                    nc.scalar.activation(wg_hi[:], wg_raw[:], ACT.Copy).then_inc(wg_split, 1)
                if split:
                    for c in range(C):
                        act.wait_ge(xt_transposed, (i - 1) * C + c + 1)
                        nc.scalar.activation(xt_hi[:, bass.ds(i - 1, 1), c, :], banks[c][:, :], ACT.Copy).then_inc(xt_hi_ready, 1)
                if gate:
                    act.wait_ge(g_projected, i - 1)
                    nc.scalar.activation(ge[:, :], banks[4][:, :], ACT.Sigmoid).then_inc(g_squashed, 1)
                if stat:
                    act.wait_ge(stat_step, i * NSTAT + NSTAT)
                    for t in range(T):
                        nc.scalar.activation(z[:, t], xin[:, s, t], ACT.Identity, bias=minus[:, t:t + 1],
                                             scale=y[:, t:t + 1]).then_inc(z_ready, 1)

            steps(act, body)
            for k in range(3):
                weights.high(act, 0, k)

        @block.tensor
        def _(pe):
            def body(i, s, stat, split, gate):
                if gate:
                    pe.wait_ge(g_squashed, i - 1)
                    if not stat:
                        pe.wait_ge(g_step, (i - 4) * NG + T)
                    for t in range(T):
                        last = nc.tensor.transpose(banks[5 + s][:, t * P:(t + 1) * P], ge[:, t * P:(t + 1) * P], m("ident"))
                    last.then_inc(g_transposed, 1)
                if stat:
                    pe.wait_ge(z_ready, i * T + T)
                    for c in range(C):
                        for t in range(T):
                            last = nc.tensor.transpose(banks[c][:, t * P:(t + 1) * P], z[:, t, c * P:(c + 1) * P], m("ident"))
                        last.then_inc(xt_transposed, 1)
                if split:
                    pe.wait_ge(xt_lo_ready, i * C)
                    for c in range(C):
                        for w, v in ((wg_hi, xt_hi), (wg_hi, xt_lo), (wg_lo, xt_hi)):
                            last = nc.tensor.matmul(banks[4][:, :], w[:, c, :], v[:, bass.ds(i - 1, 1), c, :],
                                                    start=(c == 0 and w is wg_hi and v is xt_hi), stop=(c == C - 1 and w is wg_lo))
                    last.then_inc(g_projected, 1)

            pe.wait_ge(misc_loaded, 16)
            pe.wait_ge(wg_split, 2)
            steps(pe, body)


def attend(nc, phase, banks, m, gates, xt_hi, xt_lo, weights, rope_d, o_dram, chunks):
    r = Region(nc, phase)
    rope = r("rope", [P, 2, N])
    s_full = [r(f"s_full{k}", [P, N]) for k in range(2)]
    s_swap = [r(f"s_swap{k}", [P, N]) for k in range(2)]
    qk_hi = [r(f"qk_hi{k}", [P, N], F32R) for k in range(2)]
    qk_lo = [r(f"qk_lo{k}", [P, N], F32R) for k in range(2)]
    cosed = [r(f"cosed{k}", [P, N]) for k in range(2)]
    vt = r("vt", [P, N])
    v_hi = r("v_hi", [P, T, HD], F32R)
    v_lo = r("v_lo", [P, T, HD], F32R)
    e1 = r("e1", [P, E1W])
    e2 = r("e2", [P, T, P + WIN])
    pt_hi = r("pt_hi", [P, PTW], F32R)
    pt_lo = r("pt_lo", [P, PTW], F32R)
    o_sb = r("o_sb", [P, N])
    max1 = r("max1", [P, T])
    neg_before = r("neg_before", [P, T])
    neg1 = r("neg1", [P, T])
    max2 = r("max2", [P, T])
    neg2 = r("neg2", [P, T])
    sc = r("sc", [P, T, NB])
    sc2 = r("sc2", [P, T, NB])
    mc = r("mc", [P, T])
    sums = r("sums", [P, 3, T])
    coef = r("coef", [P, 3, T])
    cb = r("cb", [P, T, NB])
    assert r.at <= nc.sbuf_usable_end, r.at

    S = nc.alloc_semaphore
    rope_loaded = S("rope_loaded")
    w_hi, w_lo, w_split = weights.hi, weights.lo, weights.split
    projected = [S(f"{k}_projected") for k in "qkv"]
    evacuated = [S(f"{k}_evacuated") for k in "qkv"]
    swapped = [S("q_swapped"), S("k_swapped")]
    cos_done = [S("q_cos"), S("k_cos")]
    sin_done = [S("q_sin"), S("k_sin")]
    roped = [S("q_roped"), S("k_roped")]
    hi_done = [S("q_hi_done"), S("k_hi_done")]
    lo_done = [S("q_lo_done"), S("k_lo_done")]
    v_transposed, v_hi_done, v_lo_done = S("v_transposed"), S("v_hi_done"), S("v_lo_done")
    scores_ready, negmax, window_masked, negmax2 = S("scores_ready"), S("negmax"), S("window_masked"), S("negmax2")
    cmp_step, exp_cmp, exp_full, exp_win = S("cmp_step"), S("exp_cmp"), S("exp_full"), S("exp_win")
    masked = S("masked")
    win_step = S("win_step")
    mixed, probs_ready = S("mixed"), S("probs_ready")
    pt_ready, pt_hi_done, pt_lo_done = S("pt_ready"), S("pt_hi_done"), S("pt_lo_done")
    out_ready, out_evacuated, out_slot_free, zeros_set = S("out_ready"), S("out_evacuated"), S("out_slot_free"), S("zeros_set")
    NC = T + 3 + 4
    QB = [4, 5, 5]

    def steps(eng, body, start=lambda h: None, spare=lambda: None):
        start(0)
        body(0, 0, True, False, False, False)
        body(1, 1, True, True, False, False)
        with eng.Fori(2, B - 1) as b:
            body(b, b, True, True, True, False)
        with eng.Fori(1, H) as h:
            body(h * B - 1, B - 1, True, True, True, h)
            start(h)
            with eng.Fori(0, B - 1) as b:
                body(h * B + b, b, True, True, True, False)
        body(H * B - 1, B - 1, True, True, True, False)
        body(H * B, None, False, True, True, False)
        spare()
        body(H * B + 1, None, False, False, True, False)

    with nc.Block() as block:
        @block.sync
        def _(sp):
            def swap(u, k):
                sp.wait_ge(evacuated[k], u + 1)
                sp.dma_start(s_swap[k][0:64, :], s_full[k][64:128, :]).then_inc(swapped[k], 16)
                sp.dma_start(s_swap[k][64:128, :], s_full[k][0:64, :]).then_inc(swapped[k], 16)

            def body(u, b, project, score, end, split):
                if split is not False:
                    weights.load(sp, split)
                if project:
                    swap(u, 0)
                    swap(u, 1)
                if end:
                    sp.wait_ge(out_evacuated, u)
                    sp.dma_start(o_dram[bass.ds(u - 2, 1)].rearrange("o p n -> p (o n)"), o_sb[:]).then_inc(out_slot_free, 16)

            sp.dma_start(rope[:].rearrange("p a n -> p (a n)"), rope_d).then_inc(rope_loaded, 16)

            def load_chunks():
                sp.wait_ge(projected[2], H * B)
                chunks.load_first(sp, 0)

            steps(sp, body, spare=load_chunks)
            sp.wait_ge(out_slot_free, 16 + 16 * H * B)

        @block.gpsimd
        def _(pool):
            def turn_cos(u, k):
                pool.wait_ge(evacuated[k], u + 1)
                nc.gpsimd.tensor_tensor(cosed[k][:], s_full[k][:], rope[:, 0, :], ALU.mult).then_inc(cos_done[k], 1)

            def turn_sin(u, k):
                pool.wait_ge(swapped[k], u * 32 + 32)
                nc.gpsimd.tensor_tensor(s_swap[k][:], s_swap[k][:], rope[:, 1, :], ALU.mult).then_inc(sin_done[k], 1)
                pool.wait_ge(cos_done[k], u + 1)
                pool.wait_ge(sin_done[k], u + 1)
                nc.gpsimd.tensor_tensor(s_full[k][:], cosed[k][:], s_swap[k][:], ALU.add).then_inc(roped[k], 1)

            def low(u, k):
                pool.wait_ge(hi_done[k], u + 1)
                nc.gpsimd.tensor_tensor(qk_lo[k][:], s_full[k][:], f32(qk_hi[k][:]), ALU.subtract).then_inc(lo_done[k], 1)

            def body(u, b, project, score, end, split):
                if project:
                    for part in (turn_cos, turn_sin, low):
                        for k in range(2):
                            part(u, k)

            nc.gpsimd.memset(o_sb[:], 0.0).then_inc(out_slot_free, 16)
            nc.gpsimd.memset(neg1[:], 0.0).then_inc(out_evacuated, 1)
            pool.wait_ge(rope_loaded, 16)
            steps(pool, body, spare=lambda: chunks.low(pool, 0, 0, 1))

        @block.tensor
        def _(pe):
            head = [0]

            def project_one(b, k):
                n = 0
                for c in range(C):
                    for w, v in ((w_hi, xt_hi), (w_hi, xt_lo), (w_lo, xt_hi)):
                        last = nc.tensor.matmul(banks[QB[k]][:, :], w[k][:, c, :], v[:, bass.ds(b, 1), c, :],
                                                start=(n == 0), stop=(n == 3 * C - 1))
                        n += 1
                last.then_inc(projected[k], 1)

            def body(u, b, project, score, end, split):
                if project:
                    pe.wait_ge(w_split[0], head[0] * 2 + 2)
                    project_one(b, 0)
                    pe.wait_ge(w_split[1], head[0] * 2 + 2)
                    if score:
                        pe.wait_ge(evacuated[2], u)
                    project_one(b, 1)
                if score:
                    pe.wait_ge(lo_done[0], u)
                    pe.wait_ge(lo_done[1], u)
                    for t in range(T):
                        w = max(256, (t + 1) * P)
                        if end:
                            pe.wait_ge(window_masked, (u - 2) * T + t + 1)
                        for n, (x, v) in enumerate(((qk_hi[0], qk_hi[1]), (qk_hi[0], qk_lo[1]), (qk_lo[0], qk_hi[1]))):
                            last = nc.tensor.matmul(banks[t][:, 0:w], x[:, t * P:(t + 1) * P], v[:, 0:w], start=(n == 0), stop=(n == 2))
                        last.then_inc(scores_ready, 1)
                if end:
                    pe.wait_ge(out_evacuated, u - 1)
                    pe.wait_ge(v_lo_done, u - 1)
                    if project:
                        pe.wait_ge(evacuated[0], u + 1)
                    pe.wait_ge(probs_ready, (u - 2) * T + T)
                    for bank, js in ((6, (0,)), (7, (1,)), (4, (2, 3))):
                        at = 0
                        for j in js:
                            for t in range(j, T):
                                last = nc.tensor.transpose(banks[bank][:, at:at + P],
                                                           e1[:, E1OFF[t] + j * P:E1OFF[t] + (j + 1) * P], m("ident"))
                                at += P
                        last.then_inc(pt_ready, 1)
                if project:
                    pe.wait_ge(w_split[2], head[0] * 2 + 2)
                    pe.wait_ge(evacuated[1], u + 1)
                    project_one(b, 2)
                if score:
                    pe.wait_ge(evacuated[2], u)
                    if end:
                        pe.wait_ge(pt_lo_done, (u - 2) * 3 + 2)
                    for t in range(T):
                        last = nc.tensor.transpose(banks[7][:, t * P:(t + 1) * P], vt[:, t * P:(t + 1) * P], m("ident"))
                    last.then_inc(v_transposed, 1)
                if end:
                    n = 0
                    for j in range(T):
                        if j < 3:
                            pe.wait_ge(pt_hi_done, (u - 2) * 3 + j + 1)
                            pe.wait_ge(pt_lo_done, (u - 2) * 3 + j + 1)
                        w = N - PTQ0[j]
                        for v, p in ((v_hi, pt_hi), (v_hi, pt_lo), (v_lo, pt_hi)):
                            last = nc.tensor.matmul(banks[6][:, PTQ0[j]:N], v[:, j, :], p[:, PTOFF[j]:PTOFF[j] + w],
                                                    start=(n == 0), stop=(n == 3 * T - 1), skip_group_check=True)
                            n += 1
                    last.then_inc(out_ready, 1)

            def start(h):
                head[0] = h

            pe.wait_ge(zeros_set, 2)
            steps(pe, body, start)

        @block.scalar
        def _(act):
            def evacuate(u, k):
                act.wait_ge(projected[k], u + 1)
                if k < 2 and not (isinstance(u, int) and u == 0):
                    act.wait_ge(lo_done[k], u)
                nc.scalar.activation((s_full[0], s_full[1], vt)[k][:], banks[QB[k]][:, :], ACT.Copy, scale=(HD ** -0.5 if k == 0 else 1.0))\
                    .then_inc(evacuated[k], 1)

            def split_weights(h, k):
                act.wait_ge(projected[k], h * B)
                weights.high(act, h, k)

            def high(u, k):
                act.wait_ge(roped[k], u + 1)
                nc.scalar.activation(qk_hi[k][:], s_full[k][:], ACT.Copy).then_inc(hi_done[k], 1)

            def body(u, b, project, score, end, split):
                for k in range(2):
                    if project:
                        evacuate(u, k)
                    if split is not False:
                        split_weights(split, k)
                if end:
                    for g in range(3):
                        w = (512, 384, 384)[g]
                        act.wait_ge(pt_ready, (u - 2) * 3 + g + 1)
                        if g < 2:
                            nc.scalar.activation(pt_hi[:, PTOFF[g]:PTOFF[g] + w], banks[6 + g][:, 0:w], ACT.Copy).then_inc(pt_hi_done, 1)
                        else:
                            nc.scalar.activation(pt_hi[:, PTOFF[2]:PTOFF[2] + 256], banks[4][:, 0:256], ACT.Copy)
                            nc.scalar.activation(pt_hi[:, PTW - P:PTW], banks[4][:, 256:384], ACT.Copy).then_inc(pt_hi_done, 1)
                if score:
                    for t in range(T):
                        w = (t + 1) * P
                        act.wait_ge(negmax, u)
                        nc.scalar.activation(e1[:, E1OFF[t]:E1OFF[t] + w], banks[t][:, 0:w], ACT.Exp, bias=neg1[:, t:t + 1],
                                             accum_out=sums[:, 1, t:t + 1]).then_inc(exp_full, 1)
                if project:
                    high(u, 0)
                    high(u, 1)
                    if score:
                        act.wait_ge(v_transposed, u)
                    evacuate(u, 2)
                if score:
                    act.wait_ge(negmax2, u)
                    for t in range(T):
                        lo = WIN if t == 0 else 0
                        nc.scalar.activation(e2[:, t, lo:], e2[:, t, lo:], ACT.Exp, bias=neg2[:, t:t + 1],
                                             accum_out=sums[:, 2, t:t + 1]).then_inc(exp_win, 1)
                        if t == 0:
                            act.wait_ge(cmp_step, (u - 1) * NC + T + 3)
                            nc.scalar.activation(sc[:], sc2[:], ACT.Exp).then_inc(exp_cmp, 1)
                if end:
                    act.wait_ge(out_ready, u - 1)
                    act.wait_ge(out_slot_free, (u - 2) * 16 + 16)
                    nc.scalar.activation(o_sb[:], banks[6][:, :], ACT.Copy).then_inc(out_evacuated, 1)
                if score:
                    act.wait_ge(v_transposed, u)
                    nc.scalar.activation(v_hi[:].rearrange("p t d -> p (t d)"), banks[7][:, :], ACT.Copy).then_inc(v_hi_done, 1)
                if split is not False:
                    split_weights(split, 2)

            steps(act, body, spare=lambda: chunks.high_first(act, 0))

        @block.vector
        def _(dve):
            def mix(t):
                nb = 2 * (t + 1)
                e = e1[:, E1OFF[t]:E1OFF[t] + nb * BS].rearrange("p (n s) -> p n s", s=BS)
                nc.vector.scalar_tensor_tensor(out=e, in0=e, scalar=coef[:, 1, t:t + 1],
                                               in1=cb[:, t, 0:nb].rearrange("p (n o) -> p n o", o=1).to_broadcast([P, nb, BS]),
                                               op0=ALU.mult, op1=ALU.add).then_inc(mixed, 1)

            def mix_window(v, t):
                lo = WIN if t == 0 else 0
                dve.wait_ge(mixed, v * T + t + 1)
                e = e1[:, E1OFF[t] + t * P - WIN + lo:E1OFF[t] + (t + 1) * P]
                nc.vector.scalar_tensor_tensor(out=e, in0=e2[:, t, lo:], scalar=coef[:, 2, t:t + 1], in1=e,
                                               op0=ALU.mult, op1=ALU.add).then_inc(probs_ready, 1)

            def body(u, b, project, score, end, split):
                v = u - 1
                if score:
                    for t in range(T):
                        diagonal = banks[t][:, t * P:(t + 1) * P]
                        dve.wait_ge(scores_ready, v * T + t + 1)
                        if t:
                            nc.vector.reduce_max(neg_before[:, t:t + 1], banks[t][:, 0:t * P], AX.X, negate=True).then_inc(masked, 1)
                        else:
                            nc.vector.memset(neg_before[:, 0:1], 3e38).then_inc(masked, 1)
                        nc.vector.tensor_tensor_reduce(out=diagonal, in0=diagonal, in1=m("causal"), scale=1.0, scalar=-3e38,
                                                       op0=ALU.add, op1=ALU.max, accum_out=max1[:, t:t + 1]).then_inc(masked, 1)
                    dve.wait_ge(masked, v * 2 * T + 2 * T)
                    nc.vector.scalar_tensor_tensor(out=neg1[:], in0=max1[:], scalar=-1.0, in1=neg_before[:],
                                                   op0=ALU.mult, op1=ALU.min).then_inc(negmax, 1)
                if end:
                    for g in range(3):
                        w = (512, 384, 384)[g]
                        dve.wait_ge(pt_hi_done, (u - 2) * 3 + g + 1)
                        if g < 2:
                            nc.vector.tensor_tensor(pt_lo[:, PTOFF[g]:PTOFF[g] + w], banks[6 + g][:, 0:w],
                                                    f32(pt_hi[:, PTOFF[g]:PTOFF[g] + w]), ALU.subtract).then_inc(pt_lo_done, 1)
                        else:
                            nc.vector.tensor_tensor(pt_lo[:, PTOFF[2]:PTOFF[2] + 256], banks[4][:, 0:256],
                                                    f32(pt_hi[:, PTOFF[2]:PTOFF[2] + 256]), ALU.subtract)
                            nc.vector.tensor_tensor(pt_lo[:, PTW - P:PTW], banks[4][:, 256:384],
                                                    f32(pt_hi[:, PTW - P:PTW]), ALU.subtract).then_inc(pt_lo_done, 1)
                if split is not False:
                    weights.low(dve, split, 0)
                    weights.low(dve, split, 1)
                if score:
                    for t in range(T):
                        nb = 2 * (t + 1)
                        dve.wait_ge(exp_full, v * T + t + 1)
                        nc.vector.reduce_sum(sc[:, t, 0:nb], banks[t][:, 0:nb * BS].rearrange("p (n s) -> p n s", s=BS),
                                             AX.X).then_inc(cmp_step, 1)
                        lo = WIN if t == 0 else 0
                        k0 = t * P - WIN + lo
                        nc.vector.tensor_tensor_reduce(out=e2[:, t, lo:], in0=banks[t][:, k0:(t + 1) * P],
                                                       in1=m("window")[:, lo:], scale=1.0, scalar=-3e38, op0=ALU.add, op1=ALU.max,
                                                       accum_out=max2[:, t:t + 1]).then_inc(window_masked, 1)
                    dve.wait_ge(window_masked, v * T + T)
                    nc.vector.tensor_scalar(neg2[:], max2[:], -1.0, None, ALU.mult).then_inc(negmax2, 1)
                    dve.wait_ge(cmp_step, v * NC + T)
                    nc.vector.scalar_tensor_tensor(out=sc2[:], in0=sc[:], scalar=1.0 / BS,
                                                   in1=m("cmask").rearrange("p (t n) -> p t n", n=NB),
                                                   op0=ALU.mult, op1=ALU.add).then_inc(cmp_step, 1)
                    dve.wait_ge(cmp_step, v * NC + T + 1)
                    nc.vector.reduce_max(mc[:], sc2[:], AX.X).then_inc(cmp_step, 1)
                if score:
                    dve.wait_ge(cmp_step, v * NC + T + 2)
                    nc.vector.tensor_tensor(sc2[:], sc2[:], mc[:].rearrange("p (t o) -> p t o", o=1).to_broadcast([P, T, NB]),
                                            ALU.subtract).then_inc(cmp_step, 1)
                    dve.wait_ge(exp_cmp, v + 1)
                    nc.vector.reduce_sum(sums[:, 0, :], sc[:], AX.X).then_inc(cmp_step, 1)
                    dve.wait_ge(cmp_step, v * NC + T + 4)
                    nc.vector.reciprocal(coef[:, 0:2], sums[:, 0:2]).then_inc(cmp_step, 1)
                    dve.wait_ge(cmp_step, v * NC + T + 5)
                    nc.vector.tensor_tensor(coef[:, 0:2], coef[:, 0:2], gates[:, bass.ds(v, 1), 0:2].rearrange("p o r t -> p (o r) t"),
                                            ALU.mult).then_inc(cmp_step, 1)
                    dve.wait_ge(cmp_step, v * NC + T + 6)
                    nc.vector.tensor_tensor(cb[:], sc[:], coef[:, 0, :].rearrange("p (t o) -> p t o", o=1).to_broadcast([P, T, NB]),
                                            ALU.mult).then_inc(cmp_step, 1)
                    dve.wait_ge(cmp_step, v * NC + T + 7)
                    for t in range(T):
                        mix(t)
                        if t == 1:
                            dve.wait_ge(exp_win, v * T + T)
                            nc.vector.reciprocal(coef[:, 2], sums[:, 2]).then_inc(win_step, 1)
                        if t == 1:
                            dve.wait_ge(v_hi_done, v + 1)
                            nc.vector.tensor_tensor(v_lo[:].rearrange("p t d -> p (t d)"), banks[7][:, :],
                                                            f32(v_hi[:].rearrange("p t d -> p (t d)")), ALU.subtract).then_inc(v_lo_done, 1)
                        if t == 2:
                            dve.wait_ge(win_step, v * 2 + 1)
                            nc.vector.tensor_tensor(coef[:, 2], coef[:, 2], gates[:, bass.ds(v, 1), 2].rearrange("p o t -> p (o t)"),
                                                    ALU.mult).then_inc(win_step, 1)
                    dve.wait_ge(win_step, v * 2 + 2)
                    for t in range(T):
                        mix_window(v, t)
                if split is not False:
                    weights.low(dve, split, 2)

            nc.vector.memset(f32(pt_hi[:, PTOFF[3]:PTOFF[3] + P]), 0.0).then_inc(zeros_set, 1)
            nc.vector.memset(f32(pt_lo[:, PTOFF[3]:PTOFF[3] + P]), 0.0).then_inc(zeros_set, 1)
            nc.vector.memset(sc[:], 0.0).then_inc(zeros_set, 1)
            dve.wait_ge(zeros_set, 3)
            steps(dve, body, spare=lambda: chunks.low_wo(dve, 0))


class Chunks:

    def __init__(self, nc, r, wo, o_dram):
        self.nc = nc
        self.G = 4
        self.K = H // self.G
        self.wo_hi, self.wo_lo = r("wo_hi", [P, H, D], F32R), r("wo_lo", [P, H, D], F32R)
        self.o_raw = [r(f"o_raw{s}", [P, self.G, N]) for s in range(2)]
        self.o_hi, self.o_lo = [None, None], [None, None]
        for s in range(2):
            self.o_hi[s], self.o_lo[s] = r(f"o_hi{s}", [P, self.G, N], F32R), r(f"o_lo{s}", [P, self.G, N], F32R)
        self.end = r.at
        self.o_v = o_dram.rearrange("(h b) p n -> p h b n", b=B)
        self.wo_v = wo.rearrange("(k g p) d -> k p g d", p=P, g=self.G)
        S = nc.alloc_semaphore
        self.raw_loaded = [S("raw_loaded0"), S("raw_loaded1")]
        self.hi_split, self.lo_split, self.chunk_used = S("hi_split"), S("lo_split"), S("chunk_used")
        self.wo_hi_split, self.wo_lo_split = S("wo_hi_split"), S("wo_lo_split")

    def load_first(self, sp, k):
        if k:
            sp.wait_ge(self.wo_lo_split, k)
        sp.dma_start(self.o_raw[0][:], self.wo_v[k]).then_inc(self.raw_loaded[0], 16)
        if k:
            sp.wait_ge(self.lo_split, k)
        sp.dma_start(self.o_raw[1][:], self.o_v[:, k * self.G:(k + 1) * self.G, 0, :]).then_inc(self.raw_loaded[1], 16)

    def high_first(self, act, k):
        act.wait_ge(self.raw_loaded[0], k * 16 + 16)
        self.nc.scalar.activation(self.wo_hi[:, k * self.G:(k + 1) * self.G, :], self.o_raw[0][:], ACT.Copy).then_inc(self.wo_hi_split, 1)
        act.wait_ge(self.raw_loaded[1], k * 16 + 16)
        if k >= 2:
            act.wait_ge(self.chunk_used, k + 1)
        self.nc.scalar.activation(self.o_hi[k % 2][:], self.o_raw[1][:], ACT.Copy).then_inc(self.hi_split, 1)

    def low_wo(self, dve, k):
        dve.wait_ge(self.wo_hi_split, k + 1)
        self.nc.vector.tensor_tensor(self.wo_lo[:, k * self.G:(k + 1) * self.G, :], self.o_raw[0][:],
                                     f32(self.wo_hi[:, k * self.G:(k + 1) * self.G, :]), ALU.subtract).then_inc(self.wo_lo_split, 1)

    def low(self, pool, b, k, slot):
        pool.wait_ge(self.hi_split, b * self.K + k + 1)
        self.nc.gpsimd.tensor_tensor(self.o_lo[k % 2][:], self.o_raw[slot][:], f32(self.o_hi[k % 2][:]),
                                     ALU.subtract).then_inc(self.lo_split, 1)


def project_and_route(nc, at, chunks, banks, m, late_d, x, wr, br, w1, b1, w2, b2, out):
    r = Region(nc, chunks.end)
    zsel_hi = r("zsel_hi", [P, C, B * P], F32R)
    zsel_lo = r("zsel_lo", [P, C, B * P], F32R)
    place = r("place", [P, B, N], F32R)
    weight = r("weight", [P, B, T])
    base_dram = nc.dram_tensor("base_scratch", [B, P, T, D], F32, kind="Internal").ap()
    G, K, wo_hi, wo_lo = chunks.G, chunks.K, chunks.wo_hi, chunks.wo_lo
    o_raw, o_hi, o_lo, o_v = chunks.o_raw, chunks.o_hi, chunks.o_lo, chunks.o_v
    raw_loaded, hi_split, lo_split, chunk_used = chunks.raw_loaded, chunks.hi_split, chunks.lo_split, chunks.chunk_used
    wo_lo_split = chunks.wo_lo_split
    xin = r("xin2", [P, T, D])
    x1 = r("x1", [P, T, D])
    z2 = r("z2", [P, T, D])
    wr_all = r("wr_all", [P, D])
    late = r("late", [P, 3 * P])
    before, slots, ones = (late[:, k * P:(k + 1) * P] for k in range(3))
    junk = r("junk", [P, D])
    diag = r("diag", [P, N])
    onehot = r("onehot", [P, T, P])
    br_all = r("br_all", [P, 1])
    stats, mv = r("stats2", [P, T, 6]), r("mv2", [P, T, 2])
    ve, sd, y, yy = (r(f"{k}_2", [P, T]) for k in ("ve", "sd", "y", "yy"))
    wraw, wcol, count, sel, unsel, selcum, slot_sb = (r(k, [P, T]) for k in ("wraw", "wcol", "count", "sel", "unsel", "selcum", "slot_sb"))
    assert r.at <= nc.sbuf_usable_end, r.at

    S = nc.alloc_semaphore
    small_loaded = S("small_loaded")
    x_loaded, acc_ready, x1_ready = S("x2_loaded"), S("acc_ready"), S("x1_ready")
    step, sd_ready, z2_ready = S("route_step"), S("sd2_ready"), S("z2_ready")
    diag_ready, row_ready, sel_ready, slot_ready = S("diag_ready"), S("row_ready"), S("sel_ready"), S("slot_ready")
    onehot_ready, zsel_ready, place_ready = S("onehot_ready"), S("zsel_ready"), S("place_ready")
    zsel_hi_done, zsel_lo_done, place_done = S("zsel_hi_done"), S("zsel_lo_done"), S("place_done")
    base_ready, base_stored = S("base_ready"), S("base_stored")
    NS = 4 + 4 + 1 + 5 + T + 1 + 1 + T + 1 + 3 + 1

    def batches(eng, body):
        with eng.Fori(0, B - 1) as b:
            body(b, True)
        body(B - 1, False)

    def wait_used(eng):
        eng.wait_ge(chunk_used, B * K + 2)

    ex_sync, ex_gpsimd, ex_scalar, ex_tensor, ex_vector = experts(
        nc, at, banks, zsel_hi, zsel_lo, place, weight, base_dram, (wait_used, zsel_lo_done, place_done, base_stored),
        w1, b1, w2, b2, out)

    with nc.Block() as block:
        @block.sync
        def _(sp):
            def load_o(b, k):
                sp.wait_ge(lo_split, b * K + k - 1)
                sp.dma_start(o_raw[k % 2][:], o_v[:, k * G:(k + 1) * G, bass.ds(b, 1), :].rearrange("p g o n -> p (g o) n"))\
                    .then_inc(raw_loaded[k % 2], 16)

            def load_x(b):
                sp.wait_ge(x1_ready, b * T + 1)
                sp.dma_start(xin[:], x[bass.ds(b, 1)].rearrange("o (t p) d -> p (o t) d", p=P)).then_inc(x_loaded, 16)

            def body(b, more):
                if more:
                    for k in range(K):
                        load_o(b + 1, k)
                        if k == 1:
                            load_x(b + 1)
                else:
                    for f in range(EARLY):
                        first(f)
                sp.wait_ge(base_ready, b * T + T)
                sp.dma_start(base_dram[bass.ds(b, 1)].rearrange("o p t d -> p (o t) d"), x1[:]).then_inc(base_stored, 16)

            for k in range(1, K):
                chunks.load_first(sp, k)
                if k == 1:
                    sp.dma_start(wr_all[:], wr.rearrange("d o -> o d").to_broadcast([P, D])).then_inc(small_loaded, 16)
                    sp.dma_start(late[:], late_d).then_inc(small_loaded, 16)
                    sp.dma_start(br_all[:], br.rearrange("(o d) -> o d", o=1).to_broadcast([P, 1])).then_inc(small_loaded, 16)
            sp.wait_ge(wo_lo_split, K)
            load_x(0)
            first, rest = ex_sync(sp)
            batches(sp, body)
            rest()

        @block.scalar
        def _(act):
            def high(b, k):
                act.wait_ge(raw_loaded[k % 2], b * 32 + (k // 2) * 16 + 48)
                act.wait_ge(chunk_used, b * K + k + 1)
                nc.scalar.activation(o_hi[k % 2][:], o_raw[k % 2][:], ACT.Copy).then_inc(hi_split, 1)

            def body(b, more):
                if more:
                    high(b + 1, 0)
                    high(b + 1, 1)
                else:
                    first(-1)
                act.wait_ge(step, b * NS + 9)
                nc.scalar.activation(sd[:], ve[:], ACT.Sqrt).then_inc(sd_ready, 1)
                if more:
                    high(b + 1, 2)
                    high(b + 1, 3)
                else:
                    for f in range(EARLY):
                        first(f)
                act.wait_ge(zsel_ready, b + 1)
                nc.scalar.activation(zsel_hi[:, :, bass.ds(b * P, P)], banks[6][:, :].rearrange("p (c s) -> p c s", c=C),
                                     ACT.Copy).then_inc(zsel_hi_done, 1)
                act.wait_ge(place_ready, b + 1)
                nc.scalar.activation(place[:, bass.ds(b, 1), :], banks[7][:, :], ACT.Copy).then_inc(place_done, 1)

            for k in range(1, K):
                chunks.high_first(act, k)
            first, rest = ex_scalar(act)
            batches(act, body)
            rest()

        @block.gpsimd
        def _(pool):
            nc.gpsimd.memset(y[:], 0.0).then_inc(chunk_used, 1)
            nc.gpsimd.memset(yy[:], 0.0).then_inc(chunk_used, 1)
            nc.gpsimd.memset(sd[:], 0.0).then_inc(x1_ready, 1)
            nc.gpsimd.memset(ve[:], 0.0).then_inc(base_stored, 16)
            for k in range(1, K):
                chunks.low(pool, 0, k, 1)
            with pool.Fori(0, B - 1) as b:
                for k in range(K):
                    chunks.low(pool, b + 1, k, k % 2)
            first, rest = ex_gpsimd(pool)
            for f in range(EARLY):
                first(f)
            rest()

        @block.tensor
        def _(pe):
            def chunk(b, k, first=False):
                pe.wait_ge(lo_split, b * K + k + 1)
                if first:
                    pe.wait_ge(wo_lo_split, k + 1)
                for t in range(T):
                    if k == 0 and not first:
                        pe.wait_ge(x1_ready, b * T + (t - 2))
                    n = 0
                    for g in range(G):
                        for o, w in ((o_hi, wo_hi), (o_hi, wo_lo), (o_lo, wo_hi)):
                            last = nc.tensor.matmul(banks[t][:, :], o[k % 2][:, g, t * P:(t + 1) * P], w[:, k * G + g, :],
                                                    start=(k == 0 and n == 0), stop=(k == K - 1 and n == 3 * G - 1))
                            n += 1
                    if k == K - 1 and t < T - 1:
                        last.then_inc(acc_ready, 1)
                last.then_inc(chunk_used, 1)

            def body(b, more):
                if more:
                    chunk(b + 1, 0)
                else:
                    pe.wait_ge(x1_ready, B * T + 1)
                    first(0)
                pe.wait_ge(diag_ready, b * T + T)
                nc.tensor.matmul(banks[4 if more else 6][:, :], ones, diag[:], start=True, stop=True).then_inc(row_ready, 1)
                if more:
                    chunk(b + 1, 1)
                else:
                    first(1)
                pe.wait_ge(sel_ready, b + 1)
                nc.tensor.matmul(banks[5 if more else 6][:, 0:T], before, sel[:], start=True, stop=False)
                nc.tensor.matmul(banks[5 if more else 6][:, 0:T], ones, selcum[:], start=False, stop=True).then_inc(slot_ready, 1)
                if more:
                    chunk(b + 1, 2)
                else:
                    first(2)
                pe.wait_ge(onehot_ready, b * T + T)
                for c in range(C):
                    for t in range(T):
                        last = nc.tensor.matmul(banks[6][:, c * P:(c + 1) * P], z2[:, t, c * P:(c + 1) * P], onehot[:, t, :],
                                                start=(t == 0), stop=(t == T - 1))
                last.then_inc(zsel_ready, 1)
                for t in range(T):
                    last = nc.tensor.transpose(banks[7][:, t * P:(t + 1) * P], onehot[:, t, :], m("ident"))
                last.then_inc(place_ready, 1)
                if more:
                    chunk(b + 1, 3)
                else:
                    first(3)

            for k in range(K):
                chunk(0, k, first=True)
            first, rest = ex_tensor(pe)
            batches(pe, body)
            rest()

        @block.vector
        def _(dve):
            v = nc.vector

            def body(b, more):
                at = [0]

                def after():
                    dve.wait_ge(step, b * NS + at[0])

                def did(ins):
                    ins.then_inc(step, 1)
                    at[0] += 1

                dve.wait_ge(x_loaded, b * 16 + 16)
                dve.wait_ge(base_stored, b * 16 + 16)
                for t in range(T):
                    if t < T - 1:
                        dve.wait_ge(acc_ready, b * (T - 1) + t + 1)
                    else:
                        dve.wait_ge(chunk_used, b * K + K + 2)
                    v.tensor_tensor(x1[:, t], xin[:, t], banks[t][:, :], ALU.add).then_inc(x1_ready, 1)
                for t in range(T):
                    dve.wait_ge(x1_ready, b * T + t + 2)
                    did(v.bn_stats(stats[:, t], x1[:, t]))
                after()
                v.memset(yy[:], 0.0)
                for t in range(T):
                    did(v.bn_aggr(mv[:, t], stats[:, t]))
                after()
                did(v.tensor_scalar(ve[:], mv[:, :, 1], EPS, None, ALU.add))
                dve.wait_ge(sd_ready, b + 1)
                did(v.reciprocal(y[:], sd[:]))
                after()
                did(v.tensor_tensor(yy[:], y[:], y[:], ALU.mult))
                after()
                did(v.tensor_tensor(yy[:], yy[:], ve[:], ALU.mult))
                after()
                did(v.tensor_scalar(yy[:], yy[:], -0.5, 1.5, ALU.mult, ALU.add))
                after()
                did(v.tensor_tensor(y[:], yy[:], y[:], ALU.mult))
                after()
                for t in range(T):
                    v.tensor_scalar(z2[:, t], x1[:, t], mv[:, t, 0:1], y[:, t:t + 1], ALU.subtract, ALU.mult).then_inc(z2_ready, 1)
                dve.wait_ge(small_loaded, 48)
                for t in range(T):
                    dve.wait_ge(z2_ready, b * T + t + 1)
                    after()
                    did(v.tensor_tensor_reduce(out=junk[:], in0=z2[:, t], in1=wr_all[:], scale=1.0, scalar=0.0,
                                               op0=ALU.mult, op1=ALU.add, accum_out=wraw[:, t:t + 1]))
                after()
                if not more:
                    first(0)
                did(v.tensor_scalar(wcol[:], wraw[:], br_all[:, 0:1], None, ALU.add))
                did(v.tensor_scalar(weight[:, bass.ds(b, 1), :], wraw[:].rearrange("p (o t) -> p o t", o=1), br_all[:, 0:1], None, ALU.add))
                after()
                for t in range(T):
                    v.tensor_scalar(diag[:, t * P:(t + 1) * P], m("ident"), wcol[:, t:t + 1], None, ALU.mult).then_inc(diag_ready, 1)
                if not more:
                    first(1)
                dve.wait_ge(row_ready, b + 1)
                for t in range(T):
                    after()
                    did(v.tensor_scalar(junk[:], banks[4 if more else 6][:, :], wcol[:, t:t + 1], None, ALU.is_ge, ALU.add,
                                        accum_out=count[:, t:t + 1]))
                after()
                did(v.tensor_scalar(sel[:], count[:], float(KTOP), None, ALU.is_lt))
                after()
                did(v.tensor_copy(selcum[:, 1:2], sel[:, 0:1]))
                v.tensor_scalar(unsel[:], sel[:], -1.0, 1.0, ALU.mult, ALU.add).then_inc(step, 1)
                at[0] += 1
                after()
                did(v.tensor_tensor(selcum[:, 2:3], selcum[:, 1:2], sel[:, 1:2], ALU.add))
                after()
                v.tensor_tensor(selcum[:, 3:4], selcum[:, 2:3], sel[:, 2:3], ALU.add).then_inc(sel_ready, 1)
                if not more:
                    first(2)
                for t in range(T):
                    v.scalar_tensor_tensor(out=x1[:, t], in0=z2[:, t], scalar=unsel[:, t:t + 1], in1=x1[:, t],
                                           op0=ALU.mult, op1=ALU.add).then_inc(base_ready, 1)
                dve.wait_ge(slot_ready, b + 1)
                did(v.tensor_copy(slot_sb[:], banks[5 if more else 6][:, 0:T]))
                after()
                for t in range(T):
                    v.tensor_scalar(onehot[:, t], slots, slot_sb[:, t:t + 1], sel[:, t:t + 1],
                                    ALU.is_equal, ALU.mult).then_inc(onehot_ready, 1)
                if not more:
                    first(3)
                dve.wait_ge(zsel_hi_done, b + 1)
                v.tensor_tensor(zsel_lo[:, :, bass.ds(b * P, P)], banks[6][:, :].rearrange("p (c s) -> p c s", c=C),
                                f32(zsel_hi[:, :, bass.ds(b * P, P)]), ALU.subtract).then_inc(zsel_lo_done, 1)
                assert at[0] == NS, (at[0], NS)

            v.memset(selcum[:], 0.0)
            for k in range(1, K):
                chunks.low_wo(dve, k)
            first, rest = ex_vector(dve)
            batches(dve, body)
            rest()


def experts(nc, at, banks, zsel_hi, zsel_lo, place, weight, base_dram, routed, w1, b1, w2, b2, out):
    wait_used, zsel_lo_done, place_done, base_stored = routed
    r = Region(nc, at)
    GB = 4
    NG = B // GB
    w1_raw, w2_raw = ([r(f"{n}{s}", [P, 512]) for s in range(2)] for n in ("w1_raw", "w2_raw"))
    w1_hi, w1_lo, w2_hi, w2_lo = ([r(f"{n}{s}", [P, 512], F32R) for s in range(2)] for n in ("w1_hi", "w1_lo", "w2_hi", "w2_lo"))
    b1_sb = r("b1_sb", [P, FT])
    b2_all = r("b2_all", [P, D])
    hid = [r(f"hid{s}", [P, GB * P]) for s in range(2)]
    hid_hi = [r(f"hid_hi{s}", [P, GB * P], F32R) for s in range(2)]
    hid_lo = [r(f"hid_lo{s}", [P, GB * P], F32R) for s in range(2)]
    ff = r("ff", [P, GB, D])
    ff_hi, ff_lo = r("ff_hi", [P, GB, D], F32R), r("ff_lo", [P, GB, D], F32R)
    NBASE = 4
    base = [r(f"base{s}", [P, T, D]) for s in range(NBASE)]
    assert r.at <= nc.sbuf_usable_end, r.at
    w1_v = w1.rearrange("(c p) f -> p c f", p=P)
    w2_v = w2.rearrange("(f p) d -> f p d", p=P)

    S = nc.alloc_semaphore
    bias_loaded = S("bias_loaded")
    w_loaded = [S("w12_loaded0"), S("w12_loaded1")]
    w1_hi_done, w1_lo_done, w2_hi_done, w2_lo_done = S("w1_hi_done"), S("w1_lo_done"), S("w2_hi_done"), S("w2_lo_done")
    hid_ready, gelu_done, hid_hi_done, hid_lo_done = S("hid_ready"), S("gelu_done"), S("hid_hi_done"), S("hid_lo_done")
    step_done, ffacc_ready, ff_ready = S("step_done"), S("ffacc_ready"), S("ff_ready")
    ff_hi_done, ff_lo_done = S("ff_hi_done"), S("ff_lo_done")
    spread_ready, final_ready = S("spread_ready"), S("final_ready")
    base_loaded = [S(f"base_loaded{s}") for s in range(NBASE)]
    stored = [S(f"stored{s}") for s in range(NBASE)]

    def spread_bank(n):
        return 6 + n % 2 if n < GB * T else 4 + n % T

    def early(f, body):
        body(f // 2, f % 2, f, f == 0, False)

    def tiles(eng, g, body):
        if g:
            for f in range(FT):
                body(g * FT // 2 + f // 2, f % 2, f, f == 0, f == FT - 1)
            return
        with eng.Fori(EARLY // 2, FT // 2 - 1) as pair:
            for s in range(2):
                body(pair, s, pair * 2 + s, False, False)
        for s in range(2):
            body(FT // 2 - 1, s, FT - 2 + s, False, s == 1)

    def sync(sp):
        def load(pair, s, f, first, last):
            if isinstance(pair, int) and pair % (FT // 2) == 0:
                return
            load_ahead(pair, s, f)

        def load_ahead(pair, s, f):
            if not (isinstance(pair, int) and pair == 0):
                sp.wait_ge(w1_lo_done, pair * 2 + s - 1)
                sp.wait_ge(w2_lo_done, pair * 2 + s - 1)
            sp.dma_start(w1_raw[s][:].rearrange("p (c f) -> p c f", c=C), w1_v[:, :, bass.ds(f * P, P)]).then_inc(w_loaded[s], 16)
            sp.dma_start(w2_raw[s][:], w2_v[bass.ds(f, 1)].rearrange("o p d -> p (o d)")).then_inc(w_loaded[s], 16)

        def load_base(n):
            b, t = divmod(n, T)
            if b >= NBASE and t == 0:
                sp.wait_ge(stored[b % NBASE], 16 * T * (b // NBASE))
            if t == 0:
                sp.wait_ge(base_stored, 16 * (b + 2))
            sp.dma_start(base[b % NBASE][:, t], base_dram[b, :, t]).then_inc(base_loaded[b % NBASE], 16)

        def store(n):
            b, t = divmod(n, T)
            sp.wait_ge(final_ready, n + 1)
            sp.dma_start(out[b, t * P:(t + 1) * P, :], base[b % NBASE][:, t]).then_inc(stored[b % NBASE], 16)

        def load_and_store(pair, s, f, first, last):
            load(pair, s, f, first, last)
            if f >= 3:
                store(f - 3)
            for n in [f + T] if f < FT // 2 else [2 * f - FT // 2 + T, 2 * f - FT // 2 + T + 1]:
                if n < (B - 2) * T:
                    load_base(n)

        def first(f):
            if f == 0:
                wait_used(sp)
                for s in range(2):
                    load_ahead(0, s, s)
                    if s == 0:
                        sp.dma_start(b1_sb[:], b1).then_inc(bias_loaded, 16)
                        sp.dma_start(b2_all[:], b2.rearrange("(o d) -> o d", o=1).to_broadcast([P, D])).then_inc(bias_loaded, 16)
            early(f, load)

        def rest():
            tiles(sp, 0, load)
            for s in range(2):
                load_ahead(FT // 2, s, s)
            for n in range(T):
                load_base(n)
            tiles(sp, 1, load_and_store)
            for n in range((B - 2) * T, (B - 1) * T):
                load_base(n)
            for n in range(FT - 3, FT):
                store(n)
            for n in range((B - 1) * T, B * T):
                load_base(n)
            for n in range(FT, B * T):
                store(n)
            for s in range(NBASE):
                sp.wait_ge(stored[s], 16 * T * (B // NBASE))

        return first, rest

    def gpsimd(pool):
        def low(pair, s, f, first, last):
            for raw, hi, lo, hi_done, lo_done in ((w1_raw, w1_hi, w1_lo, w1_hi_done, w1_lo_done),
                                                  (w2_raw, w2_hi, w2_lo, w2_hi_done, w2_lo_done)):
                pool.wait_ge(hi_done, pair * 2 + s + 1)
                nc.gpsimd.tensor_tensor(lo[s][:], raw[s][:], f32(hi[s][:]), ALU.subtract).then_inc(lo_done, 1)

        def rest():
            for g in range(NG):
                tiles(pool, g, low)

        return lambda f: early(f, low), rest

    def scalar(act):
        def high(which, pair, s):
            raw, hi, done = ((w1_raw, w1_hi, w1_hi_done), (w2_raw, w2_hi, w2_hi_done))[which]
            act.wait_ge(w_loaded[s], pair * 32 + 32)
            if not (isinstance(pair, int) and pair == 0):
                act.wait_ge((hid_ready, step_done)[which], pair * 2 + s - 1)
            nc.scalar.activation(hi[s][:], raw[s][:], ACT.Copy).then_inc(done, 1)

        def body(pair, s, f, first, last):
            nxt = (pair + s, 1 - s)
            end = last and pair == B * P * FT // (GB * P) // 2 - 1
            if not end:
                high(0, *nxt)
            act.wait_ge(hid_ready, pair * 2 + s + 1)
            nc.scalar.activation(hid[s][:], banks[4 + s][:, :], ACT.Gelu_apprx_tanh, bias=b1_sb[:, bass.ds(f, 1)]).then_inc(gelu_done, 1)
            act.wait_ge(gelu_done, pair * 2 + s + 1)
            nc.scalar.activation(hid_hi[s][:], hid[s][:], ACT.Copy).then_inc(hid_hi_done, 1)
            if not end:
                high(1, *nxt)

        def split_rows(g):
            for q in range(GB):
                act.wait_ge(ff_ready, g * GB + q + 1)
                nc.scalar.activation(ff_hi[:, q], ff[:, q], ACT.Copy).then_inc(ff_hi_done, 1)

        def body_and_rows(pair, s, f, first, last):
            body(pair, s, f, first, last)
            if first:
                split_rows(0)

        def first(f):
            if f < 0:
                act.wait_ge(bias_loaded, 32)
                high(0, 0, 0)
                high(1, 0, 0)
            else:
                early(f, body)

        def rest():
            tiles(act, 0, body)
            tiles(act, 1, body_and_rows)
            split_rows(1)

        return first, rest

    def tensor(pe):
        def hidden(g, pair, s):
            pe.wait_ge(w1_lo_done, pair * 2 + s + 1)
            k = 0
            for c in range(C):
                for w, z in ((w1_hi, zsel_hi), (w1_hi, zsel_lo), (w1_lo, zsel_hi)):
                    last = nc.tensor.matmul(banks[4 + s][:, :], w[s][:, c * P:(c + 1) * P], z[:, c, g * GB * P:(g + 1) * GB * P],
                                            start=(k == 0), stop=(k == 3 * C - 1))
                    k += 1
            last.then_inc(hid_ready, 1)

        def spread(b, t):
            n = b * T + t
            pe.wait_ge(ff_lo_done, b + 1)
            if n >= 2:
                pe.wait_ge(final_ready, n - (T - 1) if n >= GB * T + T else min(n - 1, GB * T))
            for k, v in enumerate((ff_hi, ff_lo)):
                last = nc.tensor.matmul(banks[spread_bank(n)][:, :], place[:, b, t * P:(t + 1) * P], v[:, b % GB],
                                        start=(k == 0), stop=(k == 1))
            last.then_inc(spread_ready, 1)

        def step(g, pair, s, f, first, last):
            if not last:
                hidden(g, pair + s, 1 - s)
            elif g + 1 < NG:
                pe.wait_ge(zsel_lo_done, B)
                pe.wait_ge(place_done, B)
                hidden(g + 1, pair + s, 1 - s)
            if g:
                for n in range(f - 1 if f else 0, f + 1 if last else f):
                    spread((g - 1) * GB + n // T, n % T)
                if first:
                    pe.wait_ge(ff_ready, g * GB)
            pe.wait_ge(w2_lo_done, pair * 2 + s + 1)
            pe.wait_ge(hid_lo_done, pair * 2 + s + 1)
            for q in range(GB):
                for k, (h, w) in enumerate(((hid_hi, w2_hi), (hid_hi, w2_lo), (hid_lo, w2_hi))):
                    ins = nc.tensor.matmul(banks[q][:, :], h[s][:, q * P:(q + 1) * P], w[s][:],
                                           start=(first and k == 0), stop=(last and k == 2))
                if last and q < GB - 1:
                    ins.then_inc(ffacc_ready, 1)
            ins.then_inc(step_done, 1)

        def first(f):
            if f == 0:
                pe.wait_ge(zsel_lo_done, GB)
                hidden(0, 0, 0)
            early(f, lambda *at: step(0, *at))

        def rest():
            tiles(pe, 0, lambda *at: step(0, *at))
            tiles(pe, 1, lambda *at: step(1, *at))
            for b in range(GB, B):
                for t in range(T):
                    spread(b, t)

        return first, rest

    def vector(dve):
        def low(pair, s, f, first, last):
            dve.wait_ge(hid_hi_done, pair * 2 + s + 1)
            nc.vector.tensor_tensor(hid_lo[s][:], hid[s][:], f32(hid_hi[s][:]), ALU.subtract).then_inc(hid_lo_done, 1)

        def rows(g):
            for q in range(GB):
                if q < GB - 1:
                    dve.wait_ge(ffacc_ready, g * (GB - 1) + q + 1)
                else:
                    dve.wait_ge(step_done, (g + 1) * FT)
                nc.vector.tensor_tensor(ff[:, q], banks[q][:, :], b2_all[:], ALU.add).then_inc(ff_ready, 1)

        def low_rows(g, q):
            dve.wait_ge(ff_hi_done, g * GB + q + 1)
            nc.vector.tensor_tensor(ff_lo[:, q], ff[:, q], f32(ff_hi[:, q]), ALU.subtract).then_inc(ff_lo_done, 1)

        def final(b, t):
            n = b * T + t
            if t == 0:
                dve.wait_ge(base_loaded[b % NBASE], 16 * T * (b // NBASE + 1))
            dve.wait_ge(spread_ready, n + 1)
            nc.vector.scalar_tensor_tensor(out=base[b % NBASE][:, t], in0=banks[spread_bank(n)][:, :], scalar=weight[:, b, t:t + 1],
                                           in1=base[b % NBASE][:, t], op0=ALU.mult, op1=ALU.add).then_inc(final_ready, 1)

        def low_and_final(pair, s, f, first, last):
            low(pair, s, f, first, last)
            if first:
                for q in range(GB):
                    low_rows(0, q)
            for n in range(f - 1 if f else 0, f + 1 if last else f):
                final(n // T, n % T)

        def rest():
            dve.wait_ge(bias_loaded, 32)
            tiles(dve, 0, low)
            rows(0)
            tiles(dve, 1, low_and_final)
            rows(1)
            low_rows(1, 0)
            for q in range(GB):
                if q + 1 < GB:
                    low_rows(1, q + 1)
                for t in range(T):
                    final(GB + q, t)

        return lambda f: early(f, low), rest

    return sync, gpsimd, scalar, tensor, vector


_INS = ["L0_attn_x", "L0_attn_Wq", "L0_attn_Wk", "L0_attn_Wv", "L0_attn_Wg", "L0_attn_Wo", "L0_ffn_W_r", "L0_ffn_b_r",
        "L0_ffn_W1", "L0_ffn_b1", "L0_ffn_W2", "L0_ffn_b2"]


def given(inputs):
    a = {n: np.ascontiguousarray(inputs[n]) for n in _INS}
    a["L0_ffn_b1"] = np.ascontiguousarray(a["L0_ffn_b1"].reshape(FT, P).T)
    a["rope"], a["misc"], a["late"] = consts()
    return a


def kernel(**inputs):
    import concourse.bacc as bacc
    from concourse.bass_utils import run_bass_kernel_spmd

    nc = bacc.Bacc("TRN2", target_bir_lowering=False, num_devices=1)
    arrays, args = {}, []
    for name, a in given(inputs).items():
        arrays[f"in_{name}"] = a
        args.append(nc.dram_tensor(f"in_{name}", a.shape, mybir.dt.from_np(a.dtype), kind="ExternalInput").ap())
    out = nc.dram_tensor("out", (B, N, D), F32, kind="ExternalOutput").ap()
    build(nc, *args, out)
    r = run_bass_kernel_spmd(nc, [arrays], core_ids=[0])
    return r.results[0]["out"]
```
